# Optimizing a Trainium2 kernel written in Bass

```python
import numpy as np
import jax
import jax.numpy as jnp

def _softmax(x, axis=-1):
    return jax.nn.softmax(x, axis=axis)

def _gelu(x):
    return jax.nn.gelu(x, approximate=True)

def _silu(x):
    return jax.nn.silu(x)

def _sigmoid(x):
    return jax.nn.sigmoid(x)

def _layernorm(x, axis=-1, eps=1e-05):
    m = jnp.mean(x, axis=axis, keepdims=True)
    v = jnp.var(x, axis=axis, keepdims=True)
    return (x - m) / jnp.sqrt(v + eps)

def _scatter_add(tgt, idx, src, axis=0):
    return tgt.at[idx].add(src)

def _segment_sum(src, seg, n):
    return jax.ops.segment_sum(src, seg, n)
kernel_name = 'mk_flamingo_gated_d1_seqx_r4_930535'

def setup_inputs(seed: int=0):
    np.random.seed(seed)
    _w = jnp.asarray

    def _rec_inputs():
        import jax
        import jax.numpy as jnp
        _rk = jax.random.key(seed)
        x = -0.0003929 + 0.9999 * jax.random.normal(jax.random.fold_in(_rk, 1), (16, 128, 1024), jnp.float32)
        _lenS = 128 - jax.random.randint(jax.random.fold_in(_rk, 7), (16,), 0, max(1, 128 // 4) + 1, jnp.int32)
        _lenS2 = 128 - jax.random.randint(jax.random.fold_in(_rk, 8), (16,), 0, max(1, 128 // 4) + 1, jnp.int32)
        _ctx_4096P = jax.random.normal(jax.random.fold_in(_rk, 11), (16, 16, 1024), jnp.float32)
        _ctx_4096c = jax.random.dirichlet(jax.random.fold_in(_rk, 511), 0.3 * jnp.ones((16,), jnp.float32), (16, 128))
        _ctx_4096t = jnp.einsum('bsk,bkd->bsd', _ctx_4096c, _ctx_4096P)
        _ctx_4096t = _ctx_4096t * jax.lax.rsqrt(jnp.mean(jnp.square(_ctx_4096t)) + 1e-12) * 0.953939
        ctx_4096 = 2.81802e-05 + 1.00001 * (_ctx_4096t + 0.3 * jax.random.normal(jax.random.fold_in(_rk, 611), (16, 128, 1024), jnp.float32))
        _g = jax.random.normal(jax.random.fold_in(_rk, 9001), (2, 1), jnp.float32)
        _g = jnp.sign(_g) * jnp.maximum(jnp.abs(_g), 1.0) + (_g == 0) * 1.0
        g_xattn = _g[0]
        g_ffn = _g[1]
        return (x, ctx_4096, g_xattn, g_ffn)
    x, ctx_4096, g_xattn, g_ffn = _rec_inputs()

    def _L0_xattn_setup():
        import jax, jax.numpy as jnp
        import numpy as np
        DIM = 128
        HEADS = 8
        DIM_HEAD = 64
        HIDDEN = HEADS * DIM_HEAD
        SCALE = DIM_HEAD ** (-0.5)
        key = jax.random.key(seed)
        ks = jax.random.split(key, 9)
        b, n = (8, 1024)
        std = 1.0 / np.sqrt(DIM)
        return {'q': jax.random.normal(ks[0], (b, DIM, n), jnp.float32), 'k': jax.random.normal(ks[1], (b, DIM, n), jnp.float32), 'v': jax.random.normal(ks[2], (b, DIM, n), jnp.float32), 'Wq': jax.random.normal(ks[3], (HIDDEN, DIM), jnp.float32) * std, 'Wk': jax.random.normal(ks[4], (HIDDEN, DIM), jnp.float32) * std, 'Wv': jax.random.normal(ks[5], (HIDDEN, DIM), jnp.float32) * std, 'Wo': jax.random.normal(ks[6], (DIM, HIDDEN), jnp.float32) * (1.0 / np.sqrt(HIDDEN)), 'bo': jax.random.normal(ks[7], (DIM,), jnp.float32) * 0.01, 'g': jnp.ones((1, DIM, 1), jnp.float32)}
    _L0_xattn_all = _L0_xattn_setup()
    _L0_xattn_in = {k: v for k, v in _L0_xattn_all.items() if k in ('Wq', 'Wk', 'Wv', 'Wo', 'bo', 'g')}
    del _L0_xattn_all

    def _L0_ffn_setup():
        import jax, jax.numpy as jnp
        import numpy as np
        EPS = 1e-05

        def _bitlinear(x, w):
            scale = jnp.mean(jnp.abs(w))
            q = jnp.round(jnp.clip(w / (scale + EPS), -1.0, 1.0))
            deq = q * scale
            return x @ deq.T
        key = jax.random.key(seed)
        k1, k2, k3, k4 = jax.random.split(key, 4)
        B, S, H, I = (4, 512, 1024, 2752)
        return {'hidden_states': jax.random.normal(k1, (B, S, H), dtype=jnp.float32), 'w_gate': jax.random.normal(k2, (I, H), dtype=jnp.float32) * 0.02, 'w_up': jax.random.normal(k3, (I, H), dtype=jnp.float32) * 0.02, 'w_down': jax.random.normal(k4, (H, I), dtype=jnp.float32) * 0.02}
    _L0_ffn_all = _L0_ffn_setup()
    _L0_ffn_in = {k: v for k, v in _L0_ffn_all.items() if k in ('w_gate', 'w_up', 'w_down')}
    del _L0_ffn_all
    return {'x': x, 'ctx_4096': ctx_4096, 'g_xattn': g_xattn, 'g_ffn': g_ffn, 'L0_xattn_Wq': _L0_xattn_in['Wq'], 'L0_xattn_Wk': _L0_xattn_in['Wk'], 'L0_xattn_Wv': _L0_xattn_in['Wv'], 'L0_xattn_Wo': _L0_xattn_in['Wo'], 'L0_xattn_bo': _L0_xattn_in['bo'], 'L0_xattn_g': _L0_xattn_in['g'], 'L0_ffn_w_gate': _L0_ffn_in['w_gate'], 'L0_ffn_w_up': _L0_ffn_in['w_up'], 'L0_ffn_w_down': _L0_ffn_in['w_down']}

def reference(x, ctx_4096, g_xattn, g_ffn, L0_xattn_Wq, L0_xattn_Wk, L0_xattn_Wv, L0_xattn_Wo, L0_xattn_bo, L0_xattn_g, L0_ffn_w_gate, L0_ffn_w_up, L0_ffn_w_down):
    import jax
    import jax.numpy as jnp

    def _L0_xattn_ref(q, k, v, Wq, Wk, Wv, Wo, bo, g):
        import jax, jax.numpy as jnp
        import numpy as np
        DIM = 128
        HEADS = 8
        DIM_HEAD = 64
        HIDDEN = HEADS * DIM_HEAD
        SCALE = DIM_HEAD ** (-0.5)
        b = q.shape[0]
        qh = jnp.einsum('bcn,oc->bon', q, Wq).reshape(b, HEADS, DIM_HEAD, -1)
        kh = jnp.einsum('bcn,oc->bon', k, Wk).reshape(b, HEADS, DIM_HEAD, -1)
        vh = jnp.einsum('bcn,oc->bon', v, Wv).reshape(b, HEADS, DIM_HEAD, -1)
        qh = jax.nn.softmax(qh, axis=-2) * SCALE
        kh = jax.nn.softmax(kh, axis=-1)
        context = jnp.einsum('bhdn,bhen->bhde', kh, vh)
        out = jnp.einsum('bhde,bhdn->bhen', context, qh)
        out = out.reshape(b, HIDDEN, -1)
        out = jnp.einsum('bcn,oc->bon', out, Wo) + bo[None, :, None]
        norm = jnp.maximum(jnp.sqrt(jnp.sum(out * out, axis=1, keepdims=True)), 1e-12)
        return out / norm * g * np.sqrt(DIM)

    def _L0_ffn_ref(hidden_states, w_gate, w_up, w_down):
        import jax, jax.numpy as jnp
        import numpy as np
        EPS = 1e-05

        def _bitlinear(x, w):
            scale = jnp.mean(jnp.abs(w))
            q = jnp.round(jnp.clip(w / (scale + EPS), -1.0, 1.0))
            deq = q * scale
            return x @ deq.T
        gate = _bitlinear(hidden_states, w_gate)
        up = _bitlinear(hidden_states, w_up)
        inter = gate * up
        out = _bitlinear(inter, w_down)
        return out
    x = x + jnp.tanh(g_xattn[0]) * _L0_xattn_ref(_layernorm(x, axis=-1), ctx_4096, ctx_4096, L0_xattn_Wq, L0_xattn_Wk, L0_xattn_Wv, L0_xattn_Wo, L0_xattn_bo, L0_xattn_g)
    x = x + jnp.tanh(g_ffn[0]) * _L0_ffn_ref(_layernorm(x, axis=-1), L0_ffn_w_gate, L0_ffn_w_up, L0_ffn_w_down)
    return x

_drawn_inputs = setup_inputs


def setup_inputs(seed=0):
    import zlib

    import numpy as np

    out = dict(_drawn_inputs(seed))
    spreads = {'L0_xattn_g': (1.0, 0.2)}
    factors = {}
    for name, (base, spread) in spreads.items():
        noise = np.random.default_rng([zlib.crc32(name.encode()), seed]).standard_normal(out[name].shape)
        drawn = base * np.exp(spread * noise) if base else spread * noise
        out[name] = jnp.asarray(drawn.astype(out[name].dtype))
    for name, factor in factors.items():
        out[name] = (out[name] * factor).astype(out[name].dtype)
    return out
```

```python
from contextlib import ExitStack

import concourse.bass as bass
from concourse import mybir

ALU = mybir.AluOpType
ACT = mybir.ActivationFunctionType
F32 = mybir.dt.float32
F32R = mybir.dt.float32r
F16 = mybir.dt.float16
F8 = mybir.dt.float8e4
AX_X = mybir.AxisListType.X
RMAX = bass.bass_isa.ReduceOp.max
RADD = bass.bass_isa.ReduceOp.add

P = 128
B, N = 16, 1024
HEADS, DH = 8, 64
HD = HEADS * DH
PAIRS = HD // P
NC = N // P
I = 2752
IC = I // P
TAIL = I - IC * P
GB = 2
T = GB * P
G = B // GB
EPS = 1e-5
Z_SCALE = 2.0 ** 10
I_SCALE = 2.0 ** -5
STAGES = 5
GATE, UP, DOWN = 0, 1, 2
CH = NC * P


class At:

    def __init__(self, reg, mul, add):
        self.reg, self.mul, self.add = reg, mul, add

    def count(self, per, n):
        if self.reg is None:
            return self.add * per + n
        assert self.add * per + n > 0
        return self.reg * (self.mul * per) + (self.add * per + n)

    def rows(self):
        if self.reg is None:
            return bass.ds(self.add * P, P)
        return bass.ds(self.reg * (self.mul * P) + self.add * P, P)


def wait(eng, sem, value):
    if isinstance(value, int) and value <= 0:
        return
    eng.wait_ge(sem, value)


def settle(eng, settled):
    eng.sem_inc(settled, 1)


def attention_slots(b):
    return [
        [("load", b), ("split_ctx", b), ("split_ctxT", b), ("ln1", b)],
        [("kt", b, 0), ("kt", b, 1), ("q32", b)],
        [("kt", b, 2), ("kt", b, 3)],
        [("kt", b, 4), ("kt", b, 5)],
        [("kt", b, 6), ("kt", b, 7), ("kmax", b), ("split_q", b)],
        [("qt", b, 0), ("qt", b, 1)],
        [("kshift", b, 0), ("qt", b, 2), ("tr", b, 0)],
        [("kshift", b, 1), ("qt", b, 3), ("tr", b, 1)],
        [("kshift", b, 2), ("kparts", b, 0), ("tr", b, 2)],
        [("kshift", b, 3), ("kparts", b, 1), ("tr", b, 3), ("ksum", b)],
        [("ctxk", b, 0), ("kparts", b, 2), ("ctxk", b, 1)],
        [("kparts", b, 3), ("ctxk", b, 2), ("ctxk", b, 3)],
        [("cscale", b), ("qt", b, 4), ("qt", b, 5)],
        [("mprod", b)],
        [("outp", b, 0), ("qt", b, 6), ("tr", b, 4)],
        [("norm", b, 0), ("qt", b, 7), ("tr", b, 5)],
        [("tr", b, 6)],
        [("tr", b, 7)],
        [("outp", b, 1)],
        [("norm", b, 1), ("ln2", b)],
        [("z", b)],
    ]


def weave(fill, slots):
    out, done = [], 0
    for i, f in enumerate(fill):
        out.append(f)
        upto = (i + 1) * len(slots) // len(fill)
        for s in slots[done:upto]:
            out += s
        done = upto
    return out


def weight_steps():
    chunks = [(m, c) for m in (GATE, UP, DOWN) for c in range(IC + 1)]
    out = []
    for m in (GATE, UP, DOWN):
        out += [("wsum", m, c) for c in range(IC + 1)] + [("wscale", m)]
        if m:
            out += [("wquant", m - 1, c) for c in range(IC + 1)]
    return out + [("wquant", DOWN, c) for c in range(IC + 1)], chunks


WEIGHT_STEPS = weight_steps()[0]
STAGED = [s for s in WEIGHT_STEPS if s[0] != "wscale"]
STAGE_OF = {s: n for n, s in enumerate(STAGED)}
SUM_ACT = [c for c in range(IC) if c % 2 == 0]

GU_STEPS = [("gu", j) for j in range(IC + 1)]
DOWN_PARTS = 6
DOWN_STEPS = [[("down", b, s) for s in range(DOWN_PARTS)] for b in range(GB)]

BOTH = attention_slots(0) + attention_slots(1)
PROLOGUE = [("consts",)] + weave(WEIGHT_STEPS, BOTH) + [("zt",)]
BODY = ([("reload", 0)] + weave(GU_STEPS + DOWN_STEPS[0] + DOWN_STEPS[1][:3], BOTH)
        + [("finish", 0), ("reload", 1), ("zt",)] + DOWN_STEPS[1][3:] + [("finish", 1)])
EPILOGUE = ([("reload", 0)] + GU_STEPS + DOWN_STEPS[0] + [("finish", 0), ("reload", 1)]
            + DOWN_STEPS[1] + [("finish", 1)])


def run(steps, order, ahead, group):
    for kind, *args in order:
        if kind not in steps:
            continue
        if kind in ("gu", "down", "reload", "finish"):
            steps[kind](group, *args)
        elif kind == "zt":
            steps[kind](ahead)
        elif kind in ("consts", "wsum", "wscale", "wquant"):
            steps[kind](*args)
        else:
            b = At(ahead.reg, ahead.mul * GB, ahead.add * GB + args[0])
            steps[kind](b, *args)


def program(eng, steps):
    run(steps, PROLOGUE, At(None, 0, 0), None)
    with eng.Fori(0, G - 1) as g:
        run(steps, BODY, At(g, 1, 1), At(g, 1, 0))
    run(steps, EPILOGUE, None, At(None, 0, G - 1))


def gated_attention_ffn(nc, x, ctxn, ctxt, wq, wk, wv, wo, bo, gx, g_xattn, g_ffn,
                        gate_w, up_w, down_w, down_tail, ident_in, out):
    x_rows = x.rearrange("b c n -> (b c) n")
    ctx_rows = ctxn.rearrange("b c n -> (b c) n")
    ctxt_rows = ctxt.rearrange("b p k c -> (b p) (k c)")
    out_rows = out.rearrange("b c n -> (b c) n")
    x2_dram = nc.dram_tensor("x2_dram", [B * P, N], F32, kind="Internal").ap()

    with ExitStack() as ctx:
        def sb(name, shape, dt=F32):
            return ctx.enter_context(nc.sbuf_tensor(name, shape, dt))

        def sem(name):
            return ctx.enter_context(nc.semaphore(name))

        ps = ctx.enter_context(nc.psum_tensor("ps", [P, 8, 512], F32))
        A0, A2, A3 = 4, 6, 7

        w_gu = sb("w_gu", [P, 2 * IC + 1, NC, P], F8)
        w_dn = sb("w_dn", [P, IC + 1, N], F8)
        inter_buf = sb("inter_buf", [P, IC * 2 * T + T], F16)
        inter = inter_buf[:, 0:IC * 2 * T].rearrange("p (j s t) -> p j s t", j=IC, s=2)
        inter_tail = inter_buf[:, IC * 2 * T:IC * 2 * T + T]
        stage = inter_buf[:, 0:STAGES * CH * 2].bitcast(F32).rearrange("p (s c) -> p s c", s=STAGES)
        zt_buf = sb("zt_buf", [P, 2 * NC * T], F16)
        zT = zt_buf[:, :].rearrange("p (s k t) -> p s k t", s=2, k=NC)
        above = zt_buf[:, 0:2 * CH].rearrange("p (s c) -> p s c", s=2)
        z_hi = sb("z_hi", [P, GB, N], F16)
        z_lo = sb("z_lo", [P, GB, N], F16)
        gate = sb("gate", [P, 2, T])
        fin = sb("fin", [P, 2, 512])
        wq_hi, wq_lo = sb("wq_hi", [P, HD], F32R), sb("wq_lo", [P, HD], F32R)
        wk_hi, wk_lo = sb("wk_hi", [P, HD], F32R), sb("wk_lo", [P, HD], F32R)
        a_hi, a_lo = sb("a_hi", [P, HEADS, P], F32R), sb("a_lo", [P, HEADS, P], F32R)
        xb = sb("xb", [P, N])
        raw = sb("raw", [P, N])
        rawT = sb("rawT", [P, N])
        in_hi, in_lo = sb("in_hi", [P, N], F32R), sb("in_lo", [P, N], F32R)
        ct_hi, ct_lo = sb("ct_hi", [P, N], F32R), sb("ct_lo", [P, N], F32R)
        kT = sb("kT", [P, NC, HD])
        c32 = kT[:, 0, :]
        k_hi_b, k_lo_b = sb("k_hi_b", [P, 2, HD], F32R), sb("k_lo_b", [P, 2, HD], F32R)
        kstat = sb("kstat", [P, HD])
        qs = sb("qs", [P, 2, HD])
        e_hi_b, e_lo_b = sb("e_hi_b", [P, PAIRS, 512], F32R), sb("e_lo_b", [P, PAIRS, 512], F32R)
        cc_hi_b, cc_lo_b = k_hi_b[:, 0, :], k_lo_b[:, 0, :]
        mt_hi_b, mt_lo_b = sb("mt_hi_b", [P, PAIRS, P], F32R), sb("mt_lo_b", [P, PAIRS, P], F32R)
        y = sb("y", [P, 512])
        sq = sb("sq", [P, 512])
        ident = sb("ident", [P, P])
        ident16 = sb("ident16", [P, P], F16)
        stats = sb("stats", [P, 2, 6])
        mv = sb("mv", [P, 4])
        neg_half = sb("neg_half", [P, 1])
        q_stat = sb("q_stat", [P, 2, 3, HEADS])
        absum = fin[:, 0, 0:3 * (IC + 1)].rearrange("p (m c) -> p m c", m=3)
        wtot = sb("wtot", [P, 6])
        wthr = sb("wthr", [P, 3, 3])
        small = sb("small", [P, 8])
        BO, GX, TX, TF, COEF_X, COEF_F, SC = range(7)

        s_load_w = [sem(f"s_stage{n}") for n in range(STAGES)]
        s_small, s_attw = sem("s_small"), sem("s_attw")
        x_in, ctx_in, ctxT_in = sem("x_in"), sem("ctx_in"), sem("ctxT_in")
        wsum_act, wsum_dve, wq_done = sem("wsum_act"), sem("wsum_dve"), sem("wq_done")
        above_done = sem("above_done")
        wsum_zero, wpart, wall, wthr_done = sem("wsum_zero"), sem("wpart"), sem("wall"), sem("wthr_done")
        attw_hi, attw_lo, a_ready, a_hi_s, a_lo_s = (sem("attw_hi"), sem("attw_lo"), sem("a_ready"),
                                                     sem("a_hi_s"), sem("a_lo_s"))
        tanh_done, coef_x, coef_f, id16 = sem("tanh_done"), sem("coef_x"), sem("coef_f"), sem("id16")
        c_hi, ct_hi_s, q_hi = sem("c_hi"), sem("ct_hi_s"), sem("q_hi")
        c_lo, ct_lo_s, q_lo = sem("c_lo"), sem("ct_lo_s"), sem("q_lo")
        ln1, q32 = sem("ln1"), sem("q32")
        kt_ready, kt_copied = sem("kt_ready"), sem("kt_copied")
        kmax_step, kmax_all = sem("kmax_step"), sem("kmax_all")
        k_shifted, k_exp = sem("k_shifted"), sem("k_exp")
        k_hi, k_lo = sem("k_hi"), sem("k_lo")
        ksum_step, ksum_all = sem("ksum_step"), sem("ksum_all")
        ctxk_done = sem("ctxk_done")
        k_rec, c_scaled, cc_hi, cc_lo = sem("k_rec"), sem("c_scaled"), sem("cc_hi"), sem("cc_lo")
        m_ready, mt_hi, mt_lo = sem("m_ready"), sem("mt_hi"), sem("mt_lo")
        qt_ready, q_max, q_shifted, q_exp = sem("qt_ready"), sem("q_max"), sem("q_shifted"), sem("q_exp")
        q_sum, q_rec, q_prob = sem("q_sum"), sem("q_rec"), sem("q_prob")
        tr_ready, e_hi, e_lo = sem("tr_ready"), sem("e_hi"), sem("e_lo")
        out_ready, y_ready, sq_ready, sqsum = sem("out_ready"), sem("y_ready"), sem("sq_ready"), sem("sqsum")
        rs_ready = sem("rs_ready")
        rs_inverse = sem("rs_inverse")
        rs_guarded, y_scaled, x2_ready = sem("rs_guarded"), sem("y_scaled"), sem("x2_ready")
        rstd1, rstd2, z_rstd = sem("rstd1"), sem("rstd2"), sem("z_rstd")
        x2_stored = sem("x2_stored")
        ln2, z32, z_hi_s, z_lo_s = sem("ln2"), sem("z32"), sem("z_hi_s"), sem("z_lo_s")
        settled = sem("settled")
        started = sem("started")
        zt_ready, zt_hi, zt_lo = sem("zt_ready"), sem("zt_hi"), sem("zt_lo")
        gu_ready, gate_copied, inter32, inter_hi, inter_lo = (
            sem("gu_ready"), sem("gate_copied"), sem("inter32"), sem("inter_hi"), sem("inter_lo"))
        down_ready, x2_back, fin_ready, out_stored = (
            sem("down_ready"), [sem(f"x2_back{h}") for h in range(2)], sem("fin_ready"),
            [sem(f"out_stored{h}") for h in range(2)])
        FIRST = 1
        J = IC + 1

        def staged(step):
            n = STAGE_OF[step]
            return n % STAGES, 16 * (n // STAGES + 1) + (16 * tails(n))

        def tails(n):
            return sum(1 for k in range(n % STAGES, n + 1, STAGES)
                       if STAGED[k] == ("wquant", DOWN, IC))

        def stage_view(step):
            kind, m, c = step
            s = staged(step)[0]
            cols = CH if c < IC or m == DOWN else NC * TAIL
            rows = P if c < IC or m != DOWN or kind == "wquant" else TAIL
            return stage[0:rows, s, 0:cols]

        def wait_stage_free(eng, n):
            if n < STAGES:
                return
            kind, m, c = STAGED[n - STAGES]
            if kind == "wquant":
                wait(eng, wq_done, sum(1 for s in STAGED[:n - STAGES + 1] if s[0] == "wquant"))
            elif c in SUM_ACT:
                wait(eng, wsum_act, sum(1 for s in STAGED[:n - STAGES + 1] if s[0] == "wsum" and s[2] in SUM_ACT))
            else:
                wait(eng, wsum_dve, sum(1 for s in STAGED[:n - STAGES + 1] if s[0] == "wsum" and s[2] not in SUM_ACT))

        def mt_psum(rows, s):
            v = ps[rows, A0:A0 + 2, :].rearrange("p a (b h c) -> p (a b) h c", b=2, h=2)
            return v[:, :, s, :]

        block = ctx.enter_context(nc.Block())

        @block.sync
        def _(sp):
            def hold(semaphore, value):
                wait(sp, semaphore, value)
                if not isinstance(value, int):
                    settle(sp, settled)

            pending = list(range(len(STAGED)))

            def load_stage():
                n = pending.pop(0)
                kind, m, c = step = STAGED[n]
                s = n % STAGES
                wait_stage_free(sp, n)
                if m == DOWN and c == IC:
                    sp.dma_start(stage[0:TAIL, s, :], down_tail).then_inc(s_load_w[s], 16)
                    if kind == "wquant":
                        sp.dma_start(stage[TAIL:P, s, :], down_tail).then_inc(s_load_w[s], 16)
                else:
                    src = (gate_w, up_w, down_w)[m]
                    v = stage_view(step)
                    sp.dma_start(v, src[:, c * CH:c * CH + v.shape[1]]).then_inc(s_load_w[s], 16)

            def consts():
                for hf in range(2):
                    sp.sem_inc(out_stored[hf], FIRST)
                sp.dma_start(kT[:, 0, :], wq).then_inc(s_attw, 16)
                sp.dma_start(kT[:, 1, :], wk).then_inc(s_attw, 16)
                sp.dma_start(kT[0:DH, 2:4, :].rearrange("p a b -> p (a b)"), wv).then_inc(s_attw, 16)
                sp.dma_start(kT[0:DH, 4:6, :].rearrange("p a b -> p (a b)"), wo).then_inc(s_attw, 16)
                sp.dma_start(ident[:, :], ident_in).then_inc(s_small, 16)
                for col, src in ((BO, bo), (GX, gx), (TX, g_xattn), (TF, g_ffn)):
                    sp.dma_start(small[:, col:col + 1], src).then_inc(s_small, 16)
                for _ in range(STAGES - 1):
                    load_stage()

            def load(bt, b):
                hold(q_hi, bt.count(1, 0))
                hold(q_lo, bt.count(1, 0))
                sp.dma_start(raw[:, :], ctx_rows[bt.rows(), :]).then_inc(ctx_in, 16)
                hold(ct_hi_s, bt.count(1, 0))
                hold(ct_lo_s, bt.count(1, 0))
                sp.dma_start(rawT[:, :], ctxt_rows[bt.rows(), :]).then_inc(ctxT_in, 16)
                hold(z_hi_s, bt.count(1, 0))
                hold(z_lo_s, bt.count(1, 0))
                sp.dma_start(xb[:, :], x_rows[bt.rows(), :]).then_inc(x_in, 16)

            def after_norm(bt, b, hf):
                if hf == 1:
                    hold(x2_ready, bt.count(2, 2))
                    sp.dma_start(x2_dram[bt.rows(), :], xb[:, :]).then_inc(x2_stored, 16)

            def reload(group, b):
                bt = At(group.reg, group.mul * GB, group.add * GB + b)
                sp.wait_ge(wpart, 3)
                for hf in range(2):
                    hold(out_stored[hf], group.count(32, FIRST + 16 * b))
                    if b == 0 and hf == 0:
                        hold(x2_stored, bt.count(16, 16 * GB))
                    sp.dma_start(fin[:, hf, :], x2_dram[bt.rows(), hf * 512:hf * 512 + 512]).then_inc(x2_back[hf], 16)

            def finish(group, b):
                bt = At(group.reg, group.mul * GB, group.add * GB + b)
                for hf in range(2):
                    hold(fin_ready, group.count(4, FIRST + 2 * b + hf + 1))
                    sp.dma_start(out_rows[bt.rows(), hf * 512:hf * 512 + 512], fin[:, hf, :]).then_inc(out_stored[hf], 16)

            def staged_step(*_):
                if pending:
                    load_stage()

            program(sp, {"consts": consts, "load": load, "norm": after_norm, "reload": reload,
                         "finish": finish, "wsum": staged_step, "wquant": staged_step})
            sp.wait_ge(x2_stored, 16 * B)
            sp.wait_ge(out_stored[0], FIRST + 32 * G)
            sp.wait_ge(out_stored[1], FIRST + 32 * G)

        @block.tensor
        def _(pe):
            def three(out_ap, a_h, a_l, b_h, b_l, start, stop):
                nc.tensor.matmul(out_ap, a_h, b_h, start=start, stop=False)
                nc.tensor.matmul(out_ap, a_h, b_l, start=False, stop=False)
                return nc.tensor.matmul(out_ap, a_l, b_h, start=False, stop=stop)

            def consts():
                pe.sem_inc(down_ready, FIRST)
                pe.wait_ge(s_attw, 64)
                for h in range(HEADS):
                    lhs = kT[0:DH, 2 + h // 4, (h % 4) * P:(h % 4) * P + P]
                    rhs = kT[0:DH, 4 + h // 4, (h % 4) * P:(h % 4) * P + P]
                    last = nc.tensor.matmul(ps[:, A0 + h // 4, (h % 4) * P:(h % 4) * P + P], lhs, rhs,
                                            start=True, stop=True)
                last.then_inc(a_ready, 1)

            def kt(bt, b, c):
                if c == 0:
                    wait(pe, c_hi, bt.count(1, 1))
                    wait(pe, c_lo, bt.count(1, 1))
                    wait(pe, attw_lo, 2)
                    wait(pe, attw_hi, 2)
                    wait(pe, a_lo_s, 1)
                if c < 2:
                    wait(pe, q_shifted, bt.count(8, c - 1))
                    if b == 0:
                        wait(pe, zt_lo, At(bt.reg, bt.mul // GB, bt.add // GB).count(2, 0))
                else:
                    wait(pe, kt_copied, bt.count(8, c - 1))
                s = slice(c * P, c * P + P)
                three(ps[:, A0 + c % 2, :], in_hi[:, s], in_lo[:, s], wk_hi[:, :], wk_lo[:, :], True,
                      True).then_inc(kt_ready, 1)

            def qt(bt, b, c):
                if c == 0:
                    wait(pe, q_hi, bt.count(1, 1))
                    wait(pe, q_lo, bt.count(1, 1))
                if c < 2:
                    wait(pe, kt_copied, bt.count(8, 7 + c))
                elif c < 4:
                    wait(pe, q_shifted, bt.count(8, c - 1))
                elif c < 6:
                    wait(pe, q_shifted, bt.count(8, c - 1))
                else:
                    wait(pe, mt_lo, bt.count(2, 2))
                    wait(pe, q_shifted, bt.count(8, c - 1))
                s = slice(c * P, c * P + P)
                three(ps[:, A0 + c % 2, :], in_hi[:, s], in_lo[:, s], wq_hi[:, :], wq_lo[:, :], True,
                      True).then_inc(qt_ready, 1)

            def tr(bt, b, c):
                wait(pe, q_prob, bt.count(8, c + 1))
                wait(pe, e_lo, bt.count(8, c))
                if c == 0 and b == 0:
                    wait(pe, zt_hi, At(bt.reg, bt.mul // GB, bt.add // GB).count(2, 0))
                if bt.reg is None and bt.add == 0 and c == 0:
                    pe.wait_ge(s_small, 80)
                for p in range(PAIRS):
                    last = nc.tensor.transpose(ps[:, A2, p * P:p * P + P], qs[:, c % 2, p * P:p * P + P],
                                               ident[:, :])
                last.then_inc(tr_ready, 1)

            def ctxk(bt, b, q):
                for c in (2 * q, 2 * q + 1):
                    if c == 0:
                        wait(pe, sq_ready, bt.count(2, 0))
                        wait(pe, y_ready, bt.count(2, 0))
                        wait(pe, ct_hi_s, bt.count(1, 1))
                        wait(pe, ct_lo_s, bt.count(1, 1))
                    wait(pe, k_hi, bt.count(8, c + 1))
                    wait(pe, k_lo, bt.count(8, c + 1))
                    s = slice(c * P, c * P + P)
                    three(ps[:, A3, :], ct_hi[:, s], ct_lo[:, s], k_hi_b[:, c % 2, :], k_lo_b[:, c % 2, :],
                          c == 0, c == NC - 1).then_inc(ctxk_done, 1)

            def mprod(bt, b):
                wait(pe, cc_hi, bt.count(1, 1))
                wait(pe, cc_lo, bt.count(1, 1))
                wait(pe, q_shifted, bt.count(8, 6))
                for p in range(PAIRS):
                    s = slice(p * P, p * P + P)
                    last = three(ps[:, A0 + p // 2, (p % 2) * 256:(p % 2) * 256 + 256],
                                 cc_hi_b[:, s], cc_lo_b[:, s],
                                 a_hi[:, 2 * p:2 * p + 2, :], a_lo[:, 2 * p:2 * p + 2, :], True, True)
                last.then_inc(m_ready, 1)

            def outp(bt, b, hf):
                wait(pe, e_hi, bt.count(8, 4 * hf + 4))
                wait(pe, e_lo, bt.count(8, 4 * hf + 4))
                if hf == 0:
                    wait(pe, mt_hi, bt.count(2, 2))
                    wait(pe, mt_lo, bt.count(2, 2))
                    wait(pe, c_scaled, bt.count(1, 1))
                else:
                    wait(pe, y_ready, bt.count(2, 1))
                    wait(pe, sq_ready, bt.count(2, 1))
                for p in range(PAIRS):
                    last = three(ps[:, A3, :], mt_hi_b[:, p, :], mt_lo_b[:, p, :], e_hi_b[:, p, :], e_lo_b[:, p, :],
                                 p == 0, p == PAIRS - 1)
                last.then_inc(out_ready, 1)

            def zt(nxt):
                for b in range(GB):
                    for s, (z, bank) in enumerate(((z_hi, A2), (z_lo, A0))):
                        if b == 0 and s == 0:
                            wait(pe, id16, 1)
                            wait(pe, e_lo, nxt.count(16, 16))
                        if b == 0 and s == 1:
                            wait(pe, q_shifted, nxt.count(16, 16))
                        wait(pe, z_lo_s, nxt.count(2, b + 1))
                        wait(pe, z_hi_s, nxt.count(2, b + 1))
                        if b:
                            wait(pe, (zt_hi, zt_lo)[s], nxt.count(2, 1))
                        flat = ps[:, bank, :].bitcast(F16)
                        for k in range(NC):
                            last = nc.tensor.transpose(flat[:, k * P:k * P + P], z[:, b, k * P:k * P + P],
                                                       ident16[:, :])
                        last.then_inc(zt_ready, 1)

            def gu(grp, j):
                if j == 0:
                    wait(pe, zt_hi, grp.count(2, 2))
                    wait(pe, zt_lo, grp.count(2, 2))
                    wait(pe, wq_done, 3 * (IC + 1))
                if j < 2:
                    wait(pe, fin_ready, grp.count(4, FIRST))
                else:
                    wait(pe, inter32, grp.count(J, j - 1))
                settle(pe, settled)
                if j < IC:
                    for s in range(2):
                        for k in range(NC):
                            for h in range(2):
                                last = nc.tensor.matmul(ps[:, j % 2, s * T:s * T + T], w_gu[:, 2 * j + s, k, :],
                                                        zT[:, h, k, :], start=(k == 0 and h == 0),
                                                        stop=(k == NC - 1 and h == 1))
                else:
                    for k in range(NC):
                        for h in range(2):
                            last = nc.tensor.matmul(ps[:, j % 2, 0:T], w_gu[:, 2 * IC, k, :], zT[:, h, k, :],
                                                    start=(k == 0 and h == 0), stop=(k == NC - 1 and h == 1))
                last.then_inc(gu_ready, 1)

            def down(grp, b, part):
                bank = 2 if b == 0 else 0
                t = slice(b * P, b * P + P)
                total = 2 * IC + 1
                for u in range(part * total // DOWN_PARTS, (part + 1) * total // DOWN_PARTS):
                    j = u // 2
                    if u == 0:
                        if b == 0:
                            wait(pe, fin_ready, grp.count(4, FIRST))
                        else:
                            wait(pe, inter32, grp.count(J, J))
                    if b == 0 and u % 2 == 0:
                        wait(pe, inter_hi, grp.count(J, j + 1))
                        wait(pe, inter_lo, grp.count(J, FIRST + j + 1))
                    lhs = inter[:, j, u % 2, t] if j < IC else inter_tail[:, t]
                    if b == 0 and u % 2 == 0 or u == 0:
                        settle(pe, settled)
                    for hf in range(2):
                        mm = nc.tensor.matmul(ps[:, bank + hf, :], lhs, w_dn[:, j, hf * 512:hf * 512 + 512],
                                              start=(u == 0), stop=(u == total - 1))
                        if u == total - 1:
                            mm.then_inc(down_ready, 1)

            program(pe, {"consts": consts, "kt": kt, "qt": qt, "tr": tr, "ctxk": ctxk, "mprod": mprod,
                         "outp": outp, "zt": zt, "gu": gu, "down": down})

        @block.scalar
        def _(act):
            def copy(out_ap, in_ap, scale=1.0):
                return nc.scalar.activation(out_ap, in_ap, ACT.Copy, scale=scale)

            def consts():
                act.wait_ge(s_attw, 64)
                copy(wq_hi[:, :], kT[:, 0, :]).then_inc(attw_hi, 1)
                copy(wk_hi[:, :], kT[:, 1, :]).then_inc(attw_hi, 1)
                act.wait_ge(a_ready, 1)
                copy(a_hi[:, :, :].rearrange("p h o -> p (h o)"),
                     ps[:, A0:A0 + 2, :].rearrange("p a c -> p (a c)")).then_inc(a_hi_s, 1)
                act.wait_ge(s_small, 80)
                nc.scalar.activation(small[:, TX:TF + 1], small[:, TX:TF + 1], ACT.Tanh).then_inc(tanh_done, 1)
                copy(ident16[:, :], ident[:, :]).then_inc(id16, 1)

            def wsum(m, c):
                if c not in SUM_ACT:
                    return
                s, n = staged(("wsum", m, c))
                act.wait_ge(s_load_w[s], n)
                act.wait_ge(wsum_zero, 1)
                done = m * len(SUM_ACT) + SUM_ACT.index(c)
                if done:
                    act.wait_ge(wsum_act, done)
                v = stage_view(("wsum", m, c))
                nc.scalar.activation(ps[:, 2:4, :].rearrange("p a c -> p (a c)"), v, ACT.Abs,
                                     accum_out=absum[:, m, c:c + 1]).then_inc(wsum_act, 1)

            def split_ctx(bt, b):
                wait(act, ctx_in, bt.count(16, 16))
                wait(act, qt_ready, bt.count(8, 0))
                copy(in_hi[:, :], raw[:, :]).then_inc(c_hi, 1)

            def split_ctxT(bt, b):
                wait(act, ctxT_in, bt.count(16, 16))
                wait(act, ctxk_done, bt.count(8, 0))
                copy(ct_hi[:, :], rawT[:, :]).then_inc(ct_hi_s, 1)

            def kt(bt, b, c):
                wait(act, kt_ready, bt.count(8, c + 1))
                if c == 0:
                    wait(act, cc_lo, bt.count(1, 0))
                    wait(act, cc_hi, bt.count(1, 0))
                    wait(act, ksum_step, bt.count(7, 0))
                    wait(act, k_lo, bt.count(8, 0))
                    wait(act, attw_lo, 2)
                copy(kT[:, c, :], ps[:, A0 + c % 2, :]).then_inc(kt_copied, 1)

            def split_q(bt, b):
                wait(act, q32, bt.count(1, 1))
                wait(act, kt_ready, bt.count(8, 8))
                copy(in_hi[:, :], raw[:, :]).then_inc(q_hi, 1)

            def kshift(bt, b, i):
                wait(act, k_shifted, bt.count(4, i + 1))
                v = kT[:, 2 * i:2 * i + 2, :].rearrange("p a c -> p (a c)")
                nc.scalar.activation(v, v, ACT.Exp).then_inc(k_exp, 1)

            def kparts(bt, b, i):
                for c in (2 * i, 2 * i + 1):
                    wait(act, k_exp, bt.count(4, i + 1))
                    wait(act, ctxk_done, bt.count(8, c - 1))
                    if c == 0:
                        wait(act, m_ready, bt.count(1, 0))
                    copy(k_hi_b[:, c % 2, :], kT[:, c, :]).then_inc(k_hi, 1)

            def cscale(bt, b):
                wait(act, c_scaled, bt.count(1, 1))
                wait(act, m_ready, bt.count(1, 0))
                copy(cc_hi_b, c32).then_inc(cc_hi, 1)

            def mprod(bt, b):
                wait(act, m_ready, bt.count(1, 1))
                wait(act, out_ready, bt.count(2, 0))
                for s in range(2):
                    r = slice(s * DH, s * DH + DH)
                    copy(mt_hi_b[r, :, :], mt_psum(r, s)).then_inc(mt_hi, 1)

            def qt(bt, b, c):
                wait(act, q_shifted, bt.count(8, c + 1))
                nc.scalar.activation(qs[:, c % 2, :], qs[:, c % 2, :], ACT.Exp).then_inc(q_exp, 1)

            def tr(bt, b, c):
                wait(act, tr_ready, bt.count(8, c + 1))
                if c % 4 == 0:
                    wait(act, out_ready, bt.count(2, c // 4))
                o = (c % 4) * P
                copy(e_hi_b[:, :, o:o + P], ps[:, A2, :].rearrange("p (a c) -> p a c", a=PAIRS)).then_inc(e_hi, 1)

            def outp(bt, b, hf):
                wait(act, out_ready, bt.count(2, hf + 1))
                wait(act, x2_ready, bt.count(2, hf))
                wait(act, s_small, 80)
                nc.scalar.activation(y[:, :], ps[:, A3, :], ACT.Identity, bias=small[:, BO:BO + 1],
                                     scale=DH ** -0.5).then_inc(y_ready, 1)
                nc.scalar.activation(sq[:, :], ps[:, A3, :], ACT.Square, bias=small[:, BO:BO + 1],
                                     scale=DH ** -0.5).then_inc(sq_ready, 1)

            def norm(bt, b, hf):
                wait(act, sqsum, bt.count(2, hf + 1))
                nc.scalar.activation(sq[:, :], sq[:, :], ACT.Sqrt).then_inc(rs_ready, 1)

            def z(bt, b):
                wait(act, z32, bt.count(1, 1))
                wait(act, zt_ready, At(bt.reg, bt.mul // GB, bt.add // GB).count(4, 0))
                copy(z_hi[:, b, :], xb[:, :]).then_inc(z_hi_s, 1)

            def zt(nxt):
                wait(act, gu_ready, nxt.count(J, 0))
                if nxt.reg is None:
                    act.wait_ge(wq_done, 3 * (IC + 1))
                for b in range(GB):
                    wait(act, zt_ready, nxt.count(4, 2 * b + 1))
                    copy(zT[:, 0, :, b * P:b * P + P],
                         ps[:, A2, :].bitcast(F16).rearrange("p (k t) -> p k t", k=NC)).then_inc(zt_hi, 1)

            def gu(grp, j):
                wait(act, gu_ready, grp.count(J, j + 1))
                wait(act, inter_lo, grp.count(J, FIRST + max(j - 1, 0)))
                if j < IC:
                    copy(gate[:, j % 2, :], ps[:, j % 2, 0:T], 1 / Z_SCALE).then_inc(gate_copied, 1)
                else:
                    copy(gate[0:TAIL, j % 2, :], ps[TAIL:2 * TAIL, j % 2, 0:T], 1 / Z_SCALE).then_inc(gate_copied, 1)
                wait(act, inter32, grp.count(J, j + 1))
                if j == 0:
                    wait(act, down_ready, grp.count(4, FIRST))
                if j < IC:
                    copy(inter[:, j, 0, :], gate[:, j % 2, :]).then_inc(inter_hi, 1)
                else:
                    copy(inter_tail[0:TAIL, :], gate[0:TAIL, j % 2, :]).then_inc(inter_hi, 1)

            program(act, {"consts": consts, "wsum": wsum, "split_ctx": split_ctx, "split_ctxT": split_ctxT,
                          "kt": kt, "split_q": split_q, "kshift": kshift, "kparts": kparts, "cscale": cscale,
                          "mprod": mprod, "qt": qt, "tr": tr, "outp": outp, "norm": norm, "z": z, "zt": zt, "gu": gu})

        @block.vector
        def _(dve):
            def minus(out_ap, a, b_ap):
                return nc.vector.tensor_tensor(out_ap, a, b_ap, ALU.subtract)

            def consts():
                dve.sem_inc(fin_ready, FIRST)
                dve.sem_inc(inter_lo, FIRST)
                nc.vector.memset(absum[:, :, :], 0.0).then_inc(wsum_zero, 1)
                dve.wait_ge(attw_hi, 2)
                minus(wq_lo[:, :], kT[:, 0, :], wq_hi[:, :]).then_inc(attw_lo, 1)
                minus(wk_lo[:, :], kT[:, 1, :], wk_hi[:, :]).then_inc(attw_lo, 1)
                dve.wait_ge(a_hi_s, 1)
                minus(a_lo[:, :, :].rearrange("p h o -> p (h o)"),
                      ps[:, A0:A0 + 2, :].rearrange("p a c -> p (a c)"),
                      a_hi[:, :, :].rearrange("p h o -> p (h o)")).then_inc(a_lo_s, 1)
                dve.wait_ge(tanh_done, 1)
                nc.vector.scalar_tensor_tensor(out=small[:, COEF_X:COEF_X + 1], in0=small[:, GX:GX + 1],
                                               scalar=float(P) ** 0.5, in1=small[:, TX:TX + 1], op0=ALU.mult,
                                               op1=ALU.mult).then_inc(coef_x, 1)

            def wsum(m, c):
                if c in SUM_ACT:
                    return
                step = ("wsum", m, c)
                s, n = staged(step)
                dve.wait_ge(s_load_w[s], n)
                if m == 0 and c == 1:
                    dve.wait_ge(wsum_zero, 1)
                v = stage_view(step)
                nc.vector.tensor_reduce(absum[0:v.shape[0], m, c:c + 1], v, AX_X, ALU.add,
                                        apply_absolute_value=True).then_inc(wsum_dve, 1)

            def wscale(m):
                dve.wait_ge(wsum_act, (m + 1) * len(SUM_ACT))
                dve.wait_ge(wsum_dve, (m + 1) * (IC + 1 - len(SUM_ACT)))
                nc.vector.tensor_reduce(wtot[:, m:m + 1], absum[:, m, :], AX_X, ALU.add).then_inc(wpart, 1)
                dve.wait_ge(wall, m + 1)
                nc.vector.tensor_scalar(wthr[:, m, 0:1], wtot[:, 3 + m:4 + m], 1.0 / (I * N), None,
                                        ALU.mult).then_inc(wthr_done, 1)
                dve.wait_ge(wthr_done, 3 * m + 1)
                nc.vector.tensor_scalar(wthr[:, m, 1:2], wthr[:, m, 0:1], EPS, 0.5, ALU.add,
                                        ALU.mult).then_inc(wthr_done, 1)
                nc.vector.tensor_scalar(wthr[:, m, 2:3], wthr[:, m, 0:1], EPS, -0.5, ALU.add,
                                        ALU.mult).then_inc(wthr_done, 1)
                if m == DOWN:
                    dve.wait_ge(wthr_done, 9)
                    nc.vector.scalar_tensor_tensor(out=small[:, SC:SC + 1], in0=wthr[:, GATE, 0:1],
                                                   scalar=-1.0 / I_SCALE, in1=wthr[:, UP, 0:1], op0=ALU.mult,
                                                   op1=ALU.mult).then_inc(coef_f, 1)
                    dve.wait_ge(coef_f, 1)
                    nc.vector.scalar_tensor_tensor(out=small[:, COEF_F:COEF_F + 1], in0=small[:, SC:SC + 1],
                                                   scalar=small[:, TF:TF + 1], in1=wthr[:, DOWN, 0:1],
                                                   op0=ALU.mult, op1=ALU.mult).then_inc(coef_f, 1)

            def wquant(m, c):
                step = ("wquant", m, c)
                s, n = staged(step)
                dve.wait_ge(s_load_w[s], n)
                dve.wait_ge(wthr_done, 3 * m + 3)
                v = stage_view(step)
                k = sum(1 for t in STAGED[:STAGE_OF[step]] if t[0] == "wquant")
                if k >= 2:
                    dve.wait_ge(wq_done, k - 1)
                ab = above[:, k % 2, 0:v.shape[1]]
                nc.vector.tensor_scalar(ab, v, wthr[:, m, 1:2], None, ALU.is_gt).then_inc(above_done, 1)
                dve.wait_ge(above_done, k + 1)
                if m == DOWN:
                    dst = w_dn[:, c, :]
                elif c < IC:
                    dst = w_gu[:, 2 * c + m, :, :].rearrange("p k i -> p (k i)")
                else:
                    dst = w_gu[:, 2 * IC, :, m * TAIL:m * TAIL + TAIL]
                    v = v.rearrange("p (k i) -> p k i", k=NC)
                    ab = ab.rearrange("p (k i) -> p k i", k=NC)
                nc.vector.scalar_tensor_tensor(out=dst, in0=v, scalar=wthr[:, m, 2:3], in1=ab, op0=ALU.is_lt,
                                               op1=ALU.subtract, saturate=False).then_inc(wq_done, 1)

            def split_ctx(bt, b):
                wait(dve, c_hi, bt.count(1, 1))
                minus(in_lo[:, :], raw[:, :], in_hi[:, :]).then_inc(c_lo, 1)

            def split_ctxT(bt, b):
                wait(dve, ct_hi_s, bt.count(1, 1))
                minus(ct_lo[:, :], rawT[:, :], ct_hi[:, :]).then_inc(ct_lo_s, 1)

            def row_stats(done, bt):
                for h in range(2):
                    nc.vector.bn_stats(stats[:, h, :], xb[:, h * 512:h * 512 + 512]).then_inc(done, 1)
                wait(dve, done, bt.count(4, 2))
                settle(dve, settled)
                nc.vector.bn_aggr(mv[:, 0:2], stats[:, :, :].rearrange("p a b -> p (a b)")).then_inc(done, 1)
                wait(dve, done, bt.count(4, 3))
                nc.vector.tensor_scalar(mv[:, 2:3], mv[:, 1:2], EPS, None, ALU.add).then_inc(done, 1)

            def ln1_(bt, b):
                wait(dve, x_in, bt.count(16, 16))
                row_stats(ln1, bt)

            def q32_(bt, b):
                wait(dve, rstd1, bt.count(1, 1))
                wait(dve, c_lo, bt.count(1, 1))
                nc.vector.tensor_scalar(raw[:, :], xb[:, :], mv[:, 0:1], mv[:, 3:4], ALU.subtract,
                                        ALU.mult).then_inc(q32, 1)

            def split_q(bt, b):
                wait(dve, q_hi, bt.count(1, 1))
                minus(in_lo[:, :], raw[:, :], in_hi[:, :]).then_inc(q_lo, 1)

            def kt(bt, b, c):
                if c == 0:
                    return
                wait(dve, kt_copied, bt.count(8, c + 1))
                if c > 1:
                    wait(dve, kmax_step, bt.count(7, c - 1))
                nc.vector.tensor_tensor(kstat[:, :], kT[:, 0, :] if c == 1 else kstat[:, :], kT[:, c, :],
                                        ALU.max).then_inc(kmax_step, 1)

            def kparts(bt, b, i):
                for c in (2 * i, 2 * i + 1):
                    wait(dve, k_hi, bt.count(8, c + 1))
                    wait(dve, ctxk_done, bt.count(8, c - 1))
                    minus(k_lo_b[:, c % 2, :], kT[:, c, :], k_hi_b[:, c % 2, :]).then_inc(k_lo, 1)

            def cscale(bt, b):
                wait(dve, ksum_all, bt.count(1, 1))
                nc.vector.reciprocal(kstat[:, :], kstat[:, :]).then_inc(k_rec, 1)
                wait(dve, k_rec, bt.count(1, 1))
                wait(dve, ctxk_done, bt.count(8, 8))
                wait(dve, ksum_step, bt.count(7, 7))
                wait(dve, k_lo, bt.count(8, 8))
                nc.vector.tensor_tensor(c32, ps[:, A3, :], kstat[:, :], ALU.mult).then_inc(c_scaled, 1)
                wait(dve, cc_hi, bt.count(1, 1))
                minus(cc_lo_b, c32, cc_hi_b).then_inc(cc_lo, 1)

            def mprod(bt, b):
                for s in range(2):
                    wait(dve, mt_hi, bt.count(2, 2))
                    r = slice(s * DH, s * DH + DH)
                    minus(mt_lo_b[r, :, :], mt_psum(r, s), mt_hi_b[r, :, :]).then_inc(mt_lo, 1)

            def per_head(ap):
                return ap.rearrange("p (h d) -> p h d", h=HEADS)

            def spread(ap):
                return ap.unsqueeze(2).broadcast_to([P, HEADS, DH])

            def qt(bt, b, c):
                wait(dve, qt_ready, bt.count(8, c + 1))
                t = ps[:, A0 + c % 2, :]
                nc.vector.tensor_reduce(q_stat[:, c % 2, 0, :], per_head(t), AX_X, ALU.max).then_inc(q_max, 1)
                wait(dve, q_max, bt.count(8, c + 1))
                wait(dve, tr_ready, bt.count(8, c - 1))
                nc.vector.tensor_tensor(per_head(qs[:, c % 2, :]), per_head(t), spread(q_stat[:, c % 2, 0, :]),
                                        ALU.subtract).then_inc(q_shifted, 1)
                if c % 4:
                    qsum(bt, c - 1)
                if c == 3 or c == NC - 1:
                    qsum(bt, c)

            def qsum(bt, c):
                wait(dve, q_exp, bt.count(8, c + 1))
                nc.vector.tensor_reduce(q_stat[:, c % 2, 1, :], per_head(qs[:, c % 2, :]), AX_X,
                                        ALU.add).then_inc(q_sum, 1)
                wait(dve, q_sum, bt.count(8, c + 1))
                wait(dve, q_prob, bt.count(8, c - 1))
                nc.vector.reciprocal(q_stat[:, c % 2, 2, :], q_stat[:, c % 2, 1, :]).then_inc(q_rec, 1)

            def tr(bt, b, c):
                wait(dve, e_hi, bt.count(8, c + 1))
                o = (c % 4) * P
                minus(e_lo_b[:, :, o:o + P], ps[:, A2, :].rearrange("p (a c) -> p a c", a=PAIRS),
                      e_hi_b[:, :, o:o + P]).then_inc(e_lo, 1)

            def norm(bt, b, hf):
                wait(dve, rs_ready, bt.count(2, hf + 1))
                nc.vector.tensor_scalar(sq[:, :], sq[:, :], 1e-12, None, ALU.max).then_inc(rs_guarded, 1)
                wait(dve, rs_guarded, bt.count(2, hf + 1))
                nc.vector.reciprocal(sq[:, :], sq[:, :]).then_inc(rs_inverse, 1)
                wait(dve, rs_inverse, bt.count(2, hf + 1))
                wait(dve, y_ready, bt.count(2, hf + 1))
                nc.vector.tensor_tensor(y[:, :], y[:, :], sq[:, :], ALU.mult).then_inc(y_scaled, 1)
                wait(dve, y_scaled, bt.count(2, hf + 1))
                wait(dve, coef_x, 1)
                v = xb[:, hf * 512:hf * 512 + 512]
                wait(dve, q32, bt.count(1, 1))
                nc.vector.scalar_tensor_tensor(out=v, in0=y[:, :], scalar=small[:, COEF_X:COEF_X + 1], in1=v,
                                               op0=ALU.mult, op1=ALU.add).then_inc(x2_ready, 1)

            def ln2_(bt, b):
                wait(dve, x2_ready, bt.count(2, 2))
                row_stats(ln2, bt)

            def z(bt, b):
                wait(dve, rstd2, bt.count(1, 1))
                nc.vector.tensor_scalar(mv[:, 2:3], mv[:, 3:4], Z_SCALE, None, ALU.mult).then_inc(z_rstd, 1)
                wait(dve, z_rstd, bt.count(1, 1))
                wait(dve, x2_stored, bt.count(16, 16))
                nc.vector.tensor_scalar(xb[:, :], xb[:, :], mv[:, 0:1], mv[:, 2:3], ALU.subtract,
                                        ALU.mult).then_inc(z32, 1)
                wait(dve, z_hi_s, bt.count(1, 1))
                minus(z_lo[:, b, :], xb[:, :], z_hi[:, b, :]).then_inc(z_lo_s, 1)

            def zt(nxt):
                wait(dve, gu_ready, nxt.count(J, 0))
                if nxt.reg is None:
                    dve.wait_ge(wq_done, 3 * (IC + 1))
                for b in range(GB):
                    wait(dve, zt_ready, nxt.count(4, 2 * b + 2))
                    nc.vector.tensor_copy(zT[:, 1, :, b * P:b * P + P],
                                          ps[:, A0, :].bitcast(F16).rearrange("p (k t) -> p k t", k=NC)
                                          ).then_inc(zt_lo, 1)

            def gu(grp, j):
                wait(dve, gate_copied, grp.count(J, j + 1))
                r = slice(0, P if j < IC else TAIL)
                other = ps[r, j % 2, T:2 * T] if j < IC else ps[r, j % 2, 0:T]
                nc.vector.scalar_tensor_tensor(out=gate[r, j % 2, :], in0=other, scalar=I_SCALE / Z_SCALE,
                                               in1=gate[r, j % 2, :], op0=ALU.mult,
                                               op1=ALU.mult).then_inc(inter32, 1)
                if j:
                    inter_low(grp, j - 1)
                if j == IC:
                    inter_low(grp, j)

            def inter_low(grp, j):
                wait(dve, inter_hi, grp.count(J, j + 1))
                if j < IC:
                    minus(inter[:, j, 1, :], gate[:, j % 2, :], inter[:, j, 0, :]).then_inc(inter_lo, 1)
                else:
                    minus(inter_tail[TAIL:2 * TAIL, :], gate[0:TAIL, j % 2, :],
                          inter_tail[0:TAIL, :]).then_inc(inter_lo, 1)

            def finish(grp, b):
                for hf in range(2):
                    wait(dve, down_ready, grp.count(4, FIRST + 2 * b + hf + 1))
                    wait(dve, x2_back[hf], grp.count(32, 16 * b + 16))
                    wait(dve, coef_f, 2)
                    nc.vector.scalar_tensor_tensor(out=fin[:, hf, :], in0=ps[:, (2 if b == 0 else 0) + hf, :],
                                                   scalar=small[:, COEF_F:COEF_F + 1], in1=fin[:, hf, :],
                                                   op0=ALU.mult, op1=ALU.add).then_inc(fin_ready, 1)

            program(dve, {"consts": consts, "wsum": wsum, "wscale": wscale, "wquant": wquant,
                          "split_ctx": split_ctx, "split_ctxT": split_ctxT, "ln1": ln1_, "q32": q32_, "kt": kt, "split_q": split_q,
                          "kparts": kparts, "cscale": cscale, "mprod": mprod, "qt": qt, "tr": tr, "norm": norm,
                          "ln2": ln2_, "z": z, "zt": zt, "gu": gu, "finish": finish})

        @block.gpsimd
        def _(pool):
            def consts():
                nc.gpsimd.memset(neg_half[:, :], -0.5).then_inc(started, 1)

            def rstd(bt, stat, done):
                wait(pool, started, 1)
                wait(pool, stat, bt.count(4, 4))
                nc.gpsimd.tensor_tensor(mv[:, 3:4], mv[:, 2:3], neg_half[:, :], ALU.pow).then_inc(done, 1)

            def ln1_(bt, b):
                rstd(bt, ln1, rstd1)

            def ln2_(bt, b):
                rstd(bt, ln2, rstd2)

            def wscale(m):
                pool.wait_ge(wpart, m + 1)
                nc.gpsimd.partition_all_reduce(wtot[:, 3 + m:4 + m], wtot[:, m:m + 1], P, RADD).then_inc(wall, 1)

            def kmax(bt, b):
                wait(pool, kmax_step, bt.count(7, 7))
                settle(pool, settled)
                nc.gpsimd.partition_all_reduce(kstat[:, :], kstat[:, :], P, RMAX).then_inc(kmax_all, 1)

            def kshift(bt, b, i):
                wait(pool, kmax_all, bt.count(1, 1))
                v = kT[:, 2 * i:2 * i + 2, :]
                nc.gpsimd.tensor_tensor(v, v, kstat[:, :].unsqueeze(1).broadcast_to([P, 2, HD]),
                                        ALU.subtract).then_inc(k_shifted, 1)

            def ksum(bt, b):
                wait(pool, k_shifted, bt.count(4, 4))
                for c in range(1, NC):
                    wait(pool, k_exp, bt.count(4, c // 2 + 1))
                    if c > 1:
                        wait(pool, ksum_step, bt.count(7, c - 1))
                    nc.gpsimd.tensor_tensor(kstat[:, :], kT[:, 0, :] if c == 1 else kstat[:, :], kT[:, c, :],
                                            ALU.add).then_inc(ksum_step, 1)
                wait(pool, ksum_step, bt.count(7, 7))
                settle(pool, settled)
                nc.gpsimd.partition_all_reduce(kstat[:, :], kstat[:, :], P, RADD).then_inc(ksum_all, 1)

            def qt(bt, b, c):
                if c % 4:
                    qprob(bt, c - 1)
                if c == 3 or c == NC - 1:
                    qprob(bt, c)

            def qprob(bt, c):
                wait(pool, q_rec, bt.count(8, c + 1))
                v = qs[:, c % 2, :].rearrange("p (h d) -> p h d", h=HEADS)
                nc.gpsimd.tensor_tensor(v, v, q_stat[:, c % 2, 2, :].unsqueeze(2).broadcast_to([P, HEADS, DH]),
                                        ALU.mult).then_inc(q_prob, 1)

            def outp(bt, b, hf):
                wait(pool, sq_ready, bt.count(2, hf + 1))
                settle(pool, settled)
                nc.gpsimd.partition_all_reduce(sq[:, :], sq[:, :], P, RADD).then_inc(sqsum, 1)

            program(pool, {"consts": consts, "ln1": ln1_, "ln2": ln2_, "wscale": wscale, "kmax": kmax, "kshift": kshift, "ksum": ksum, "qt": qt,
                           "outp": outp})


def kernel(**inputs):
    import numpy as np
    import concourse.bacc as bacc
    from concourse.bass_utils import run_bass_kernel_spmd

    nc = bacc.Bacc("TRN2", target_bir_lowering=False, num_devices=1)
    f = {k: np.asarray(v) for k, v in inputs.items()}

    def chunked(w):
        t = w.T.reshape(NC, P, I).transpose(1, 0, 2)
        full = t[:, :, :IC * P].reshape(P, NC, IC, P).transpose(0, 2, 1, 3).reshape(P, IC * CH)
        return np.concatenate([full, t[:, :, IC * P:].reshape(P, NC * TAIL)], axis=1)

    down_t = f["L0_ffn_w_down"].T
    arrays = {
        "x": f["x"],
        "ctxn": f["ctx_4096"],
        "ctxt": f["ctx_4096"].transpose(0, 2, 1).reshape(B, NC, P, P).transpose(0, 2, 1, 3),
        "wq": f["L0_xattn_Wq"].T,
        "wk": f["L0_xattn_Wk"].T,
        "wv": f["L0_xattn_Wv"].reshape(HEADS, DH, P).transpose(1, 0, 2).reshape(DH, HEADS * P),
        "wo": f["L0_xattn_Wo"].T.reshape(HEADS, DH, P).transpose(1, 0, 2).reshape(DH, HEADS * P),
        "bo": f["L0_xattn_bo"].reshape(P, 1),
        "gx": f["L0_xattn_g"].reshape(P, 1),
        "g_xattn": np.broadcast_to(f["g_xattn"].reshape(1, 1), (P, 1)),
        "g_ffn": np.broadcast_to(f["g_ffn"].reshape(1, 1), (P, 1)),
        "gate_w": chunked(f["L0_ffn_w_gate"]),
        "up_w": chunked(f["L0_ffn_w_up"]),
        "down_w": down_t[:IC * P].reshape(IC, P, N).transpose(1, 0, 2).reshape(P, IC * N),
        "down_tail": down_t[IC * P:],
        "ident": np.eye(P, dtype=np.float32),
    }
    arrays = {f"in_{k}": np.ascontiguousarray(v) for k, v in arrays.items()}
    args = [nc.dram_tensor(k, v.shape, mybir.dt.from_np(v.dtype), kind="ExternalInput").ap()
            for k, v in arrays.items()]
    args.append(nc.dram_tensor("out", (B, P, N), F32, kind="ExternalOutput").ap())
    gated_attention_ffn(nc, *args)
    r = run_bass_kernel_spmd(nc, [arrays], core_ids=[0])
    return r.results[0]["out"]
```

```python
from contextlib import ExitStack

import concourse.bass as bass
from concourse import mybir

ALU = mybir.AluOpType
ACT = mybir.ActivationFunctionType
F32 = mybir.dt.float32
F32R = mybir.dt.float32r
F16 = mybir.dt.float16
F8 = mybir.dt.float8e4
AX_X = mybir.AxisListType.X
RMAX = bass.bass_isa.ReduceOp.max
RADD = bass.bass_isa.ReduceOp.add

P = 128
B, N = 16, 1024
HEADS, DH = 8, 64
HD = HEADS * DH
PAIRS = HD // P
NC = N // P
I = 2752
IC = I // P
TAIL = I - IC * P
GB = 2
T = GB * P
G = B // GB
EPS = 1e-5
Z_SCALE = 2.0 ** 10
I_SCALE = 2.0 ** -5
QR = 4
STAGES = 12
GATE, UP, DOWN = 0, 1, 2
CH = NC * P


class At:

    def __init__(self, reg, mul, add):
        self.reg, self.mul, self.add = reg, mul, add

    def count(self, per, n):
        if self.reg is None:
            return self.add * per + n
        assert self.add * per + n > 0
        return self.reg * (self.mul * per) + (self.add * per + n)

    def rows(self):
        if self.reg is None:
            return bass.ds(self.add * P, P)
        return bass.ds(self.reg * (self.mul * P) + self.add * P, P)


def wait(eng, sem, value):
    if isinstance(value, int) and value <= 0:
        return
    eng.wait_ge(sem, value)


def settle(eng, settled):
    eng.sem_inc(settled, 1)


def attention_slots():
    at = [
        ("load", [0]),
        ("split_ctx", [1]),
        ("kcopy", [3, 3, 4, 4, 5, 5, 6, 6]),
        ("ln1", [3]),
        ("kmax", [7]),
        ("q32", [7]),
        ("split_q", [8]),
        ("split_ctxT", [8]),
        ("nroot", [28, 33]),
        ("nrec", [29, 34]),
        ("norm", [30, 35]),
        ("ln2", [36]),
        ("z", [38]),
        ("y", [26, 31]),
        ("e", [13, 14, 16, 17, 26, 27, 28, 29]),
        ("kshift", [9, 10, 12, 13]),
        ("qsub", [10, 11, 13, 14, 16, 18, 20, 21]),
        ("qsum", [10, 11, 13, 14, 16, 18, 21, 22]),
        ("kparts", [11, 12, 13, 14, 15, 16, 17, 18]),
        ("kexp", [10, 11, 13, 14]),
        ("ksum", [14, 15, 16, 17, 17, 18, 19]),
        ("cparts", [20]),
        ("ztotal", [21]),
        ("mparts", [23]),
        ("kt", [2, 2, 3, 3, 4, 4, 5, 5]),
        ("tr", [12, 13, 15, 16]),
        ("ctxk", [12, 13, 14, 15, 16, 17, 18, 19]),
        ("zsum", [21]),
        ("mprod", [22]),
        ("outp", [25, 31]),
        ("qt", [8, 9, 11, 12, 14, 16, 18, 19]),
        ("tr_late", [25, 26, 27, 28]),
    ]
    slots = [[] for _ in range(1 + max(max(v) for _, v in at))]
    for kind, starts in at:
        for i, slot in enumerate(starts):
            if kind == "tr_late":
                slots[slot].append(("tr", 4 + i))
            else:
                slots[slot].append((kind, i))
    return slots


PRO_SLOTS = 64
LAG = 20


def weave(fill, slots=65):
    one = attention_slots()
    both = [[] for _ in range(slots)]
    for b in range(GB):
        for n, steps in enumerate(one):
            both[n + b * LAG] += [(kind, b, i) for kind, i in steps]
    out, done = [], 0
    for i, f in enumerate(fill):
        out += f
        upto = (i + 1) * slots // len(fill)
        for s in both[done:upto]:
            out += s
        done = upto
    return out


def sums(m):
    steps = [[("wsum", m, c)] for c in range(IC + 1)]
    steps[-1].append(("wscale", m))
    return steps


def quants(m):
    steps = [[("wquant", m, c)] + ([("wsign", m, c - 1)] if c else []) for c in range(IC + 1)]
    steps[-1].append(("wsign", m, IC))
    return steps


GU_WEIGHTS = sums(GATE) + sums(UP) + quants(GATE) + quants(UP)
DOWN_WEIGHTS = sums(DOWN) + quants(DOWN)
STAGED = [s for steps in GU_WEIGHTS + DOWN_WEIGHTS for s in steps if s[0] in ("wsum", "wquant")]
STAGE_OF = {s: n for n, s in enumerate(STAGED)}
DOWN_QUANT_SLOTS = [10, 11, 7, 8, 9, 10, 11, 7, 8, 9, 10, 11, 9, 10, 11, 9, 10, 11, 10, 11, 10, 11]
SLOT = [n % 10 if m != DOWN else 5 + c % 5 if kind == "wsum" else DOWN_QUANT_SLOTS[c]
        for n, (kind, m, c) in enumerate(STAGED)]
BEFORE = [max([k for k in range(n) if SLOT[k] == SLOT[n]], default=-1) for n in range(len(STAGED))]
SUM_ACT = [c for c in range(IC) if c % 3 != 0]
ROUND = 1.5 * 2.0 ** 23

DOWN_PARTS = 12
DOWN_STEPS = [[[("down", b, s)] for s in range(DOWN_PARTS)] for b in range(GB)]
FFN_STEPS = [[("gu", 0, 0)], [("gu", 0, 1)]]
for _j in range(1, IC):
    FFN_STEPS += [[("gu", _j, 0)], [("inter", _j - 1), ("gu", _j, 1)]]
FFN_STEPS += [[("gu", IC, 0), ("inter", IC - 1)], DOWN_STEPS[0][0] + [("inter", IC)]]
FFN_STEPS += DOWN_STEPS[0][1:] + DOWN_STEPS[1]
DOWN_WEIGHTS_END = 38
GU_END, DOWN0_END = 2 * IC + 1, 2 * IC + 1 + DOWN_PARTS

FFN_STEPS[DOWN0_END] = FFN_STEPS[DOWN0_END] + [("finish", 0), ("reload", 1)]
FFN_STEPS[0] = [("reload", 0)] + FFN_STEPS[0]
FFN_STEPS[-1] = FFN_STEPS[-1] + [("finish", 1)]
ZT_AT = {GU_END + 2: ("zt", 0), len(FFN_STEPS) - 3: ("zt", 1)}
PROLOGUE = [("consts",)] + weave(GU_WEIGHTS, slots=PRO_SLOTS) + [("zt", 0), ("zt", 1)]
BODY = weave([f + [ZT_AT[i]] if i in ZT_AT else f for i, f in enumerate(FFN_STEPS)])
FIRST_STEPS = [list(f) for f in FFN_STEPS]
for _i, _steps in enumerate(DOWN_WEIGHTS):
    FIRST_STEPS[_i * DOWN_WEIGHTS_END // len(DOWN_WEIGHTS)] += _steps
FIRST_STEPS[0].remove(("reload", 0))
FIRST_STEPS[GU_END].append(("reload", 0))
FIRST_BODY = weave([f + [ZT_AT[i]] if i in ZT_AT else f for i, f in enumerate(FIRST_STEPS)])
EPILOGUE = [s for f in FFN_STEPS for s in f]


def run(steps, order, ahead, group):
    for kind, *args in order:
        if kind not in steps:
            continue
        if kind in ("gu", "inter", "down", "reload", "finish"):
            steps[kind](group, *args)
        elif kind == "zt":
            steps[kind](ahead, *args)
        elif kind in ("consts", "wsum", "wscale", "wquant", "wsign"):
            steps[kind](*args)
        else:
            b = At(ahead.reg, ahead.mul * GB, ahead.add * GB + args[0])
            steps[kind](b, *args)


def program(eng, steps):
    run(steps, PROLOGUE, At(None, 0, 0), None)
    run(steps, FIRST_BODY, At(None, 0, 1), At(None, 0, 0))
    with eng.Fori(0, G - 2) as g:
        run(steps, BODY, At(g, 1, 2), At(g, 1, 1))
    run(steps, EPILOGUE, None, At(None, 0, G - 1))


def gated_attention_ffn(nc, x, ctxn, ctxt, wq, wk, wv, wo, bo, gx, g_xattn, g_ffn,
                        gate_w, up_w, down_w, down_tail, ident_in, out):
    x_rows = x.rearrange("b c n -> (b c) n")
    ctx_rows = ctxn.rearrange("b c n -> (b c) n")
    ctxt_rows = ctxt.rearrange("b p k c -> (b p) (k c)")
    out_rows = out.rearrange("b c n -> (b c) n")
    x2_dram = nc.dram_tensor("x2_dram", [B * P, N], F32, kind="Internal").ap()

    with ExitStack() as ctx:
        def sb(name, shape, dt=F32):
            return ctx.enter_context(nc.sbuf_tensor(name, shape, dt))

        def overlaid(name, low_name, shape):
            with nc.sbuf_tensor(name, shape, F32) as whole:
                pass
            return whole, sb(low_name, shape, F32R)

        def sem(name):
            return ctx.enter_context(nc.semaphore(name))

        ps = ctx.enter_context(nc.psum_tensor("ps", [P, 8, 512], F32))
        A0, A2, A3 = 4, 6, 7
        ZT_BANKS = ((0, 1), (A2, A0))

        w_gu = sb("w_gu", [P, 2 * IC + 1, NC, P], F8)
        w_dn = sb("w_dn", [P, IC + 1, N], F8)
        inter_buf = sb("inter_buf", [P, IC * 2 * T + T], F16)
        inter = inter_buf[:, 0:IC * 2 * T].rearrange("p (j s t) -> p j s t", j=IC, s=2)
        inter_tail = inter_buf[:, IC * 2 * T:IC * 2 * T + T]
        stage_a = inter_buf[:, 0:5 * CH * 2].bitcast(F32).rearrange("p (s c) -> p s c", s=5)
        stage_b = w_dn[:, 0:5 * 4, :].rearrange("p j n -> p (j n)").bitcast(F32).rearrange("p (s c) -> p s c", s=5)
        zt_buf = sb("zt_buf", [P, 2 * NC * T], F16)
        zT = zt_buf[:, :].rearrange("p (s k t) -> p s k t", s=2, k=NC)
        z_hi = sb("z_hi", [P, GB, N], F16)
        z_lo = sb("z_lo", [P, GB, N], F16)
        gate = sb("gate", [P, 2, T])
        fin = sb("fin", [P, 2, 512])
        wq_hi, wq_lo = sb("wq_hi", [P, HD], F32R), sb("wq_lo", [P, HD], F32R)
        wk_hi, wk_lo = sb("wk_hi", [P, HD], F32R), sb("wk_lo", [P, HD], F32R)
        a_hi, a_lo = sb("a_hi", [P, HEADS, P], F32R), sb("a_lo", [P, HEADS, P], F32R)
        xb_ring = sb("xb_ring", [P, GB, N])
        in_hi, (raw, in_lo) = sb("in_hi", [P, N], F32R), overlaid("raw", "in_lo", [P, N])
        ct_hi, (rawT, ct_lo) = sb("ct_hi", [P, N], F32R), overlaid("rawT", "ct_lo", [P, N])
        kT = sb("kT", [P, NC, HD])
        k_hi_b, k_lo_b = sb("k_hi_b", [P, 2, HD], F32R), sb("k_lo_b", [P, 2, HD], F32R)
        kstat = sb("kstat", [P, HD])
        qs = sb("qs", [P, QR, HD])
        e_hi_b, e_lo_b = sb("e_hi_b", [P, PAIRS, 512], F32R), sb("e_lo_b", [P, PAIRS, 512], F32R)
        cc_hi_b, cc_lo_b = k_hi_b[:, 0, :], k_lo_b[:, 0, :]
        mt_hi_b, (m32, mt_lo_b) = sb("mt_hi_b", [P, PAIRS, P], F32R), overlaid("m32", "mt_lo_b", [P, PAIRS, P])
        y = sb("y", [P, 512])
        sq = sb("sq", [P, 512])
        ident = sb("ident", [P, P])
        ident16 = sb("ident16", [P, P], F16)
        stats = sb("stats", [P, 2, 6])
        mv = sb("mv", [P, 4])
        mv2 = sb("mv2", [P, 4])
        q_stat = sb("q_stat", [P, QR, 2, HEADS])
        cst = sb("cst", [P, 7])
        neg_half, ones, minus_round, k_rec_b = cst[:, 0:1], cst[:, 1:2], cst[:, 2:3], cst[:, 3:3 + PAIRS]
        absum = fin[:, 0, 0:3 * (IC + 1)].rearrange("p (m c) -> p m c", m=3)
        wtot = sb("wtot", [P, 3])
        wthr = sb("wthr", [P, 3, 3])
        small = sb("small", [P, 7])
        BO, GX, TX, TF, COEF_X, COEF_F, SC = range(7)

        s_load_w = [sem(f"s_stage{n}") for n in range(STAGES)]
        s_small, s_attw = sem("s_small"), sem("s_attw")
        x_in, ctx_in, ctxT_in = sem("x_in"), sem("ctx_in"), sem("ctxT_in")
        wsum_act, wsum_dve, wq_done = sem("wsum_act"), sem("wsum_dve"), sem("wq_done")
        w_rounded, round_set = sem("w_rounded"), sem("round_set")
        wsum_zero, wpart, wall, wthr_done = sem("wsum_zero"), sem("wpart"), sem("wall"), sem("wthr_done")
        attw_hi, attw_lo, a_ready, a_hi_s, a_lo_s = (sem("attw_hi"), sem("attw_lo"), sem("a_ready"),
                                                     sem("a_hi_s"), sem("a_lo_s"))
        tanh_done, coef_x, coef_f, id16 = sem("tanh_done"), sem("coef_x"), sem("coef_f"), sem("id16")
        c_hi, ct_hi_s, q_hi = sem("c_hi"), sem("ct_hi_s"), sem("q_hi")
        c_lo, ct_lo_s, q_lo = sem("c_lo"), sem("ct_lo_s"), sem("q_lo")
        ln1, q32 = sem("ln1"), sem("q32")
        kt_ready, kt_copied = sem("kt_ready"), sem("kt_copied")
        kmax_step, kmax_all = sem("kmax_step"), sem("kmax_all")
        k_shifted, k_exp = sem("k_shifted"), sem("k_exp")
        k_hi, k_lo = sem("k_hi"), sem("k_lo")
        ksum_step = sem("ksum_step")
        ctxk_done = sem("ctxk_done")
        denom_ready, k_rec, cc_hi, cc_lo = sem("denom_ready"), sem("k_rec"), sem("cc_hi"), sem("cc_lo")
        m_ready, m_scaled, mt_hi, mt_lo = sem("m_ready"), sem("m_scaled"), sem("mt_hi"), sem("mt_lo")
        qt_ready, q_max, q_shifted, q_exp = sem("qt_ready"), sem("q_max"), sem("q_shifted"), sem("q_exp")
        q_sum, q_rec, q_prob = sem("q_sum"), sem("q_rec"), sem("q_prob")
        tr_ready, e_hi, e_lo = sem("tr_ready"), sem("e_hi"), sem("e_lo")
        out_ready, y_ready, sq_ready, sqsum = sem("out_ready"), sem("y_ready"), sem("sq_ready"), sem("sqsum")
        rs_ready = sem("rs_ready")
        rs_inverse = sem("rs_inverse")
        rs_guarded, y_scaled, x2_ready = sem("rs_guarded"), sem("y_scaled"), sem("x2_ready")
        rstd1, rstd2, z_rstd = sem("rstd1"), sem("rstd2"), sem("z_rstd")
        x2_stored = sem("x2_stored")
        ln2, z32, z_hi_s, z_lo_s = sem("ln2"), sem("z32"), sem("z_hi_s"), sem("z_lo_s")
        settled = sem("settled")
        started = sem("started")
        zt_ready, zt_hi, zt_lo = sem("zt_ready"), sem("zt_hi"), sem("zt_lo")
        gu_ready, gate_copied, inter32, inter_hi, inter_lo = (
            sem("gu_ready"), sem("gate_copied"), sem("inter32"), sem("inter_hi"), sem("inter_lo"))
        down_ready, x2_back, fin_ready, out_stored = (
            sem("down_ready"), [sem(f"x2_back{h}") for h in range(2)], sem("fin_ready"),
            [sem(f"out_stored{h}") for h in range(2)])
        J = IC + 1

        def staged(step):
            n = STAGE_OF[step]
            loads = [STAGED[k] for k in range(n + 1) if SLOT[k] == SLOT[n]]
            return SLOT[n], 16 * (len(loads) + loads.count(("wquant", DOWN, IC)))

        def stage_slot(s, rows, cols):
            if s >= 10:
                return (z_hi, z_lo)[s - 10][rows, :, :].rearrange("p b n -> p (b n)").bitcast(F32)[:, cols]
            return stage_a[rows, s, cols] if s < 5 else stage_b[rows, s - 5, cols]

        def stage_view(step):
            kind, m, c = step
            cols = CH if c < IC or m == DOWN else NC * TAIL
            rows = P if c < IC or m != DOWN or kind == "wquant" else TAIL
            return stage_slot(SLOT[STAGE_OF[step]], slice(0, rows), slice(0, cols))

        def wait_stage_free(eng, n):
            n = BEFORE[n]
            if n < 0:
                return
            kind, m, c = STAGED[n]
            if kind == "wquant":
                wait(eng, wq_done, sum(1 for s in STAGED[:n + 1] if s[0] == "wquant"))
            elif c in SUM_ACT:
                wait(eng, wsum_act, sum(1 for s in STAGED[:n + 1] if s[0] == "wsum" and s[2] in SUM_ACT))
            else:
                wait(eng, wsum_dve, sum(1 for s in STAGED[:n + 1] if s[0] == "wsum" and s[2] not in SUM_ACT))

        def mt_psum(rows, s):
            v = ps[rows, A2:A2 + 2, :].rearrange("p a (b h c) -> p (a b) h c", b=2, h=2)
            return v[:, :, s, :]

        block = ctx.enter_context(nc.Block())

        @block.sync
        def _(sp):
            def hold(semaphore, value):
                wait(sp, semaphore, value)
                if not isinstance(value, int):
                    settle(sp, settled)

            pending = list(range(len(STAGED)))

            def load_stages(k):
                while pending and BEFORE[pending[0]] < max(k - 1, 0) and pending[0] <= 2 * k + 3:
                    load_stage()

            def load_stage():
                n = pending.pop(0)
                if SLOT[n] >= 10:
                    wait(sp, zt_ready, 4)
                kind, m, c = step = STAGED[n]
                s = SLOT[n]
                wait_stage_free(sp, n)
                if m == DOWN and c == IC:
                    sp.dma_start(stage_slot(s, slice(0, TAIL), slice(0, CH)), down_tail).then_inc(s_load_w[s], 16)
                    if kind == "wquant":
                        sp.dma_start(stage_slot(s, slice(TAIL, P), slice(0, CH)), down_tail).then_inc(s_load_w[s], 16)
                else:
                    src = (gate_w, up_w, down_w)[m]
                    v = stage_view(step)
                    sp.dma_start(v, src[:, c * CH:c * CH + v.shape[1]]).then_inc(s_load_w[s], 16)

            def consts():
                sp.dma_start(kT[:, 0, :], wq).then_inc(s_attw, 16)
                sp.dma_start(kT[:, 1, :], wk).then_inc(s_attw, 16)
                sp.dma_start(kT[0:DH, 2:4, :].rearrange("p a b -> p (a b)"), wv).then_inc(s_attw, 16)
                sp.dma_start(kT[0:DH, 4:6, :].rearrange("p a b -> p (a b)"), wo).then_inc(s_attw, 16)
                sp.dma_start(ident[:, :], ident_in).then_inc(s_small, 16)
                for col, src in ((BO, bo), (GX, gx), (TX, g_xattn), (TF, g_ffn)):
                    sp.dma_start(small[:, col:col + 1], src).then_inc(s_small, 16)
                for _ in range(3):
                    load_stage()

            def load(bt, b, _):
                hold(qt_ready, bt.count(8, 0))
                sp.dma_start(raw[:, :], ctx_rows[bt.rows(), :]).then_inc(ctx_in, 16)
                hold(z_hi_s, bt.count(1, -1))
                hold(z_lo_s, bt.count(1, -1))
                sp.dma_start(xb_ring[:, b, :], x_rows[bt.rows(), :]).then_inc(x_in, 16)
                hold(ctxk_done, bt.count(8, 0))
                sp.dma_start(rawT[:, :], ctxt_rows[bt.rows(), :]).then_inc(ctxT_in, 16)

            def after_norm(bt, b, hf):
                if hf == 1:
                    hold(x2_ready, bt.count(2, 2))
                    sp.dma_start(x2_dram[bt.rows(), :], xb_ring[:, b, :]).then_inc(x2_stored, 16)

            def reload(group, b):
                bt = At(group.reg, group.mul * GB, group.add * GB + b)
                sp.wait_ge(wpart, 3)
                for hf in range(2):
                    hold(out_stored[hf], group.count(32, 16 * b))
                    if b == 0 and hf == 0:
                        hold(x2_stored, bt.count(16, 16 * GB))
                    sp.dma_start(fin[:, hf, :], x2_dram[bt.rows(), hf * 512:hf * 512 + 512]).then_inc(x2_back[hf], 16)

            def finish(group, b):
                bt = At(group.reg, group.mul * GB, group.add * GB + b)
                for hf in range(2):
                    hold(fin_ready, group.count(4, 2 * b + hf + 1))
                    sp.dma_start(out_rows[bt.rows(), hf * 512:hf * 512 + 512], fin[:, hf, :]).then_inc(out_stored[hf], 16)

            def wsum(m, c):
                load_stages(STAGE_OF[("wsum", m, c)])

            def wquant(m, c):
                load_stages(STAGE_OF[("wquant", m, c)])

            program(sp, {"consts": consts, "load": load, "norm": after_norm, "reload": reload,
                         "finish": finish, "wsum": wsum, "wquant": wquant})
            sp.wait_ge(x2_stored, 16 * B)
            sp.wait_ge(out_stored[0], 32 * G)
            sp.wait_ge(out_stored[1], 32 * G)

        @block.tensor
        def _(pe):
            def three(out_ap, a_h, a_l, b_h, b_l, start, stop):
                nc.tensor.matmul(out_ap, a_h, b_h, start=start, stop=False)
                nc.tensor.matmul(out_ap, a_h, b_l, start=False, stop=False)
                return nc.tensor.matmul(out_ap, a_l, b_h, start=False, stop=stop)

            def consts():
                pe.wait_ge(s_attw, 64)
                for h in range(HEADS):
                    lhs = kT[0:DH, 2 + h // 4, (h % 4) * P:(h % 4) * P + P]
                    rhs = kT[0:DH, 4 + h // 4, (h % 4) * P:(h % 4) * P + P]
                    last = nc.tensor.matmul(ps[:, A0 + h // 4, (h % 4) * P:(h % 4) * P + P], lhs, rhs,
                                            start=True, stop=True)
                last.then_inc(a_ready, 1)

            def kt(bt, b, c):
                if c == 0:
                    wait(pe, c_hi, bt.count(1, 1))
                    wait(pe, c_lo, bt.count(1, 1))
                    wait(pe, attw_lo, 2)
                    wait(pe, attw_hi, 2)
                    wait(pe, a_lo_s, 1)
                if c < 2:
                    wait(pe, q_shifted, bt.count(8, c - 1))
                    if b == 0:
                        wait(pe, zt_lo, At(bt.reg, bt.mul // GB, bt.add // GB).count(2, 0))
                else:
                    wait(pe, kt_copied, bt.count(8, c - 1))
                s = slice(c * P, c * P + P)
                three(ps[:, A0 + c % 2, :], in_hi[:, s], in_lo[:, s], wk_hi[:, :], wk_lo[:, :], True,
                      True).then_inc(kt_ready, 1)

            def qt(bt, b, c):
                if c == 0:
                    wait(pe, q_hi, bt.count(1, 1))
                    wait(pe, q_lo, bt.count(1, 1))
                if c < 2:
                    wait(pe, kt_copied, bt.count(8, 7 + c))
                else:
                    wait(pe, q_shifted, bt.count(8, c - 1))
                s = slice(c * P, c * P + P)
                three(ps[:, A0 + c % 2, :], in_hi[:, s], in_lo[:, s], wq_hi[:, :], wq_lo[:, :], True,
                      True).then_inc(qt_ready, 1)

            def tr(bt, b, c):
                wait(pe, q_prob, bt.count(8, c + 1))
                wait(pe, e_lo, bt.count(8, c))
                if c == 0 and b == 0:
                    wait(pe, zt_hi, At(bt.reg, bt.mul // GB, bt.add // GB).count(2, 0))
                if c == 4:
                    wait(pe, m_scaled, bt.count(2, 2))
                if bt.reg is None and bt.add == 0 and c == 0:
                    pe.wait_ge(s_small, 80)
                for p in range(PAIRS):
                    last = nc.tensor.transpose(ps[:, A2, p * P:p * P + P], qs[:, c % QR, p * P:p * P + P],
                                               ident[:, :])
                last.then_inc(tr_ready, 1)

            def ctxk(bt, b, c):
                if c == 0:
                    wait(pe, sq_ready, bt.count(2, 0))
                    wait(pe, y_ready, bt.count(2, 0))
                    wait(pe, ct_hi_s, bt.count(1, 1))
                    wait(pe, ct_lo_s, bt.count(1, 1))
                wait(pe, k_hi, bt.count(8, c + 1))
                wait(pe, k_lo, bt.count(8, c + 1))
                s = slice(c * P, c * P + P)
                three(ps[:, A3, :], ct_hi[:, s], ct_lo[:, s], k_hi_b[:, c % 2, :], k_lo_b[:, c % 2, :],
                      c == 0, c == NC - 1).then_inc(ctxk_done, 1)

            def zsum(bt, b, _):
                wait(pe, started, 2)
                wait(pe, ksum_step, bt.count(7, 7))
                wait(pe, e_hi, bt.count(8, 4))
                wait(pe, e_lo, bt.count(8, 4))
                for p in range(PAIRS):
                    last = nc.tensor.matmul(ps[:, A2, p:p + 1], kstat[:, p * P:p * P + P], ones[:, :],
                                            start=True, stop=True)
                last.then_inc(denom_ready, 1)

            def mprod(bt, b, _):
                wait(pe, cc_hi, bt.count(1, 1))
                wait(pe, cc_lo, bt.count(1, 1))
                wait(pe, k_rec, bt.count(1, 1))
                for p in range(PAIRS):
                    s = slice(p * P, p * P + P)
                    last = three(ps[:, A2 + p // 2, (p % 2) * 256:(p % 2) * 256 + 256],
                                 cc_hi_b[:, s], cc_lo_b[:, s],
                                 a_hi[:, 2 * p:2 * p + 2, :], a_lo[:, 2 * p:2 * p + 2, :], True, True)
                last.then_inc(m_ready, 1)

            def outp(bt, b, hf):
                wait(pe, e_hi, bt.count(8, 4 * hf + 4))
                wait(pe, e_lo, bt.count(8, 4 * hf + 4))
                if hf == 0:
                    wait(pe, mt_hi, bt.count(2, 2))
                    wait(pe, mt_lo, bt.count(2, 2))
                else:
                    wait(pe, y_ready, bt.count(2, 1))
                    wait(pe, sq_ready, bt.count(2, 1))
                for p in range(PAIRS):
                    last = three(ps[:, A3, :], mt_hi_b[:, p, :], mt_lo_b[:, p, :], e_hi_b[:, p, :], e_lo_b[:, p, :],
                                 p == 0, p == PAIRS - 1)
                last.then_inc(out_ready, 1)

            def zt(nxt, b):
                for s, z in enumerate((z_hi, z_lo)):
                    if b == 0:
                        wait(pe, id16, 1)
                        wait(pe, inter32, nxt.count(J, 0))
                    elif s == 0:
                        wait(pe, e_lo, nxt.count(16, 16))
                        wait(pe, e_hi, nxt.count(16, 16))
                    else:
                        wait(pe, q_shifted, nxt.count(16, 16))
                    wait(pe, (z_hi_s, z_lo_s)[s], nxt.count(2, b + 1))
                    flat = ps[:, ZT_BANKS[b][s], :].bitcast(F16)
                    for k in range(NC):
                        last = nc.tensor.transpose(flat[:, k * P:k * P + P], z[:, b, k * P:k * P + P],
                                                   ident16[:, :])
                    last.then_inc(zt_ready, 1)

            def gu(grp, j, s):
                if j == 0 and s == 0:
                    wait(pe, zt_hi, grp.count(2, 2))
                    wait(pe, zt_lo, grp.count(2, 2))
                    wait(pe, wq_done, 2 * (IC + 1))
                if s == 0:
                    if j < 2:
                        wait(pe, fin_ready, grp.count(4, 0))
                    else:
                        wait(pe, inter32, grp.count(J, j - 1))
                    settle(pe, settled)
                w = 2 * j + s
                for k in range(NC):
                    for h in range(2):
                        last = nc.tensor.matmul(ps[:, j % 2, s * T:s * T + T], w_gu[:, w, k, :], zT[:, h, k, :],
                                                start=(k == 0 and h == 0), stop=(k == NC - 1 and h == 1))
                if s == 1 or j == IC:
                    last.then_inc(gu_ready, 1)

            def down(grp, b, part):
                bank = 2 if b == 0 else 0
                t = slice(b * P, b * P + P)
                total = 2 * IC + 1
                for u in range(part * total // DOWN_PARTS, (part + 1) * total // DOWN_PARTS):
                    j = u // 2
                    if u == 0:
                        if b == 0:
                            wait(pe, wq_done, 3 * (IC + 1))
                            wait(pe, fin_ready, grp.count(4, 0))
                        else:
                            wait(pe, inter32, grp.count(J, J))
                            if grp.reg is not None or grp.add < G - 1:
                                wait(pe, zt_hi, grp.count(2, 3))
                                wait(pe, zt_lo, grp.count(2, 3))
                    if b == 0 and u % 2 == 0:
                        wait(pe, inter_hi, grp.count(J, j + 1))
                        wait(pe, inter_lo, grp.count(J, j + 1))
                    lhs = inter[:, j, u % 2, t] if j < IC else inter_tail[:, t]
                    if b == 0 and u % 2 == 0 or u == 0:
                        settle(pe, settled)
                    for hf in range(2):
                        mm = nc.tensor.matmul(ps[:, bank + hf, :], lhs, w_dn[:, j, hf * 512:hf * 512 + 512],
                                              start=(u == 0), stop=(u == total - 1))
                        if u == total - 1:
                            mm.then_inc(down_ready, 1)

            program(pe, {"consts": consts, "kt": kt, "qt": qt, "tr": tr, "ctxk": ctxk, "zsum": zsum, "mprod": mprod,
                         "outp": outp, "zt": zt, "gu": gu, "down": down})

        @block.scalar
        def _(act):
            def copy(out_ap, in_ap, scale=1.0):
                return nc.scalar.activation(out_ap, in_ap, ACT.Copy, scale=scale)

            def consts():
                act.wait_ge(s_attw, 64)
                copy(wq_hi[:, :], kT[:, 0, :]).then_inc(attw_hi, 1)
                copy(wk_hi[:, :], kT[:, 1, :]).then_inc(attw_hi, 1)
                act.wait_ge(a_ready, 1)
                copy(a_hi[:, :, :].rearrange("p h o -> p (h o)"),
                     ps[:, A0:A0 + 2, :].rearrange("p a c -> p (a c)")).then_inc(a_hi_s, 1)
                act.wait_ge(s_small, 80)
                nc.scalar.activation(small[:, TX:TF + 1], small[:, TX:TF + 1], ACT.Tanh).then_inc(tanh_done, 1)
                copy(ident16[:, :], ident[:, :]).then_inc(id16, 1)

            def wsum(m, c):
                if c not in SUM_ACT:
                    return
                s, n = staged(("wsum", m, c))
                act.wait_ge(s_load_w[s], n)
                act.wait_ge(wsum_zero, 1)
                done = m * len(SUM_ACT) + SUM_ACT.index(c)
                if done:
                    act.wait_ge(wsum_act, done)
                v = stage_view(("wsum", m, c))
                nc.scalar.activation(ps[:, 2:4, :].rearrange("p a c -> p (a c)"), v, ACT.Abs,
                                     accum_out=absum[:, m, c:c + 1]).then_inc(wsum_act, 1)

            def wsign(m, c):
                act.wait_ge(w_rounded, m * (IC + 1) + c + 1)
                act.wait_ge(round_set, 1)
                v = stage_view(("wquant", m, c))
                if m == DOWN:
                    act.wait_ge(wq_done, 2 * (IC + 1) + c)
                if m == DOWN:
                    dst = w_dn[:, c, :]
                elif c < IC:
                    dst = w_gu[:, 2 * c + m, :, :].rearrange("p k i -> p (k i)")
                else:
                    dst = w_gu[:, 2 * IC, :, m * TAIL:m * TAIL + TAIL]
                    v = v.rearrange("p (k i) -> p k i", k=NC)
                nc.scalar.activation(dst, v, ACT.Sign, bias=minus_round, saturate=False).then_inc(wq_done, 1)

            def split_ctx(bt, b, _):
                wait(act, ctx_in, bt.count(16, 16))
                wait(act, qt_ready, bt.count(8, 0))
                copy(in_hi[:, :], raw[:, :]).then_inc(c_hi, 1)

            def split_ctxT(bt, b, _):
                wait(act, ctxT_in, bt.count(16, 16))
                wait(act, ctxk_done, bt.count(8, 0))
                copy(ct_hi[:, :], rawT[:, :]).then_inc(ct_hi_s, 1)

            def kcopy(bt, b, c):
                wait(act, kt_ready, bt.count(8, c + 1))
                if c == 0:
                    wait(act, ksum_step, bt.count(7, 0))
                    wait(act, k_lo, bt.count(8, 0))
                    wait(act, k_hi, bt.count(8, 0))
                    wait(act, attw_lo, 2)
                copy(kT[:, c, :], ps[:, A0 + c % 2, :]).then_inc(kt_copied, 1)

            def split_q(bt, b, _):
                wait(act, q32, bt.count(1, 1))
                wait(act, kt_ready, bt.count(8, 8))
                copy(in_hi[:, :], raw[:, :]).then_inc(q_hi, 1)

            def kexp(bt, b, i):
                wait(act, k_shifted, bt.count(4, i + 1))
                v = kT[:, 2 * i:2 * i + 2, :].rearrange("p a c -> p (a c)")
                nc.scalar.activation(v, v, ACT.Exp).then_inc(k_exp, 1)

            def kparts(bt, b, c):
                wait(act, k_exp, bt.count(4, c // 2 + 1))
                wait(act, ctxk_done, bt.count(8, c - 1))
                if c == 0:
                    wait(act, m_ready, bt.count(1, 0))
                copy(k_hi_b[:, c % 2, :], kT[:, c, :]).then_inc(k_hi, 1)

            def cparts(bt, b, _):
                wait(act, ctxk_done, bt.count(8, 8))
                copy(cc_hi_b, ps[:, A3, :]).then_inc(cc_hi, 1)

            def mparts(bt, b, _):
                for s in range(2):
                    wait(act, m_scaled, bt.count(2, s + 1))
                    wait(act, out_ready, bt.count(2, 0))
                    r = slice(s * DH, s * DH + DH)
                    copy(mt_hi_b[r, :, :], m32[r, :, :]).then_inc(mt_hi, 1)

            def qsub(bt, b, c):
                wait(act, q_shifted, bt.count(8, c + 1))
                nc.scalar.activation(qs[:, c % QR, :], qs[:, c % QR, :], ACT.Exp).then_inc(q_exp, 1)

            def e(bt, b, c):
                wait(act, tr_ready, bt.count(8, c + 1))
                if c % 4 == 0:
                    wait(act, out_ready, bt.count(2, c // 4))
                o = (c % 4) * P
                copy(e_hi_b[:, :, o:o + P], ps[:, A2, :].rearrange("p (a c) -> p a c", a=PAIRS)).then_inc(e_hi, 1)

            def y_(bt, b, hf):
                wait(act, out_ready, bt.count(2, hf + 1))
                wait(act, x2_ready, bt.count(2, hf))
                wait(act, s_small, 80)
                nc.scalar.activation(y[:, :], ps[:, A3, :], ACT.Identity, bias=small[:, BO:BO + 1],
                                     scale=DH ** -0.5).then_inc(y_ready, 1)
                nc.scalar.activation(sq[:, :], ps[:, A3, :], ACT.Square, bias=small[:, BO:BO + 1],
                                     scale=DH ** -0.5).then_inc(sq_ready, 1)

            def nroot(bt, b, hf):
                wait(act, sqsum, bt.count(2, hf + 1))
                nc.scalar.activation(sq[:, :], sq[:, :], ACT.Sqrt).then_inc(rs_ready, 1)

            def z(bt, b, _):
                wait(act, z32, bt.count(1, 1))
                if bt.reg is None and bt.add >= GB:
                    act.wait_ge(wq_done, 3 * (IC + 1))
                wait(act, zt_ready, At(bt.reg, bt.mul // GB, bt.add // GB).count(4, 2 * b - 2))
                copy(z_hi[:, b, :], xb_ring[:, b, :]).then_inc(z_hi_s, 1)

            def zt(nxt, b):
                wait(act, gu_ready, nxt.count(J, 0))
                wait(act, zt_ready, nxt.count(4, 2 * b + 1))
                copy(zT[:, 0, :, b * P:b * P + P],
                     ps[:, ZT_BANKS[b][0], :].bitcast(F16).rearrange("p (k t) -> p k t", k=NC)).then_inc(zt_hi, 1)

            def inter_(grp, j):
                wait(act, gu_ready, grp.count(J, j + 1))
                wait(act, inter_lo, grp.count(J, max(j - 1, 0)))
                if j < IC:
                    copy(gate[:, j % 2, :], ps[:, j % 2, 0:T], 1 / Z_SCALE).then_inc(gate_copied, 1)
                else:
                    copy(gate[0:TAIL, j % 2, :], ps[TAIL:2 * TAIL, j % 2, 0:T], 1 / Z_SCALE).then_inc(gate_copied, 1)
                if j:
                    inter_high(grp, j - 1)
                if j == IC:
                    inter_high(grp, j)

            def inter_high(grp, j):
                wait(act, inter32, grp.count(J, j + 1))
                if j == 0:
                    wait(act, down_ready, grp.count(4, 0))
                if j < IC:
                    copy(inter[:, j, 0, :], gate[:, j % 2, :]).then_inc(inter_hi, 1)
                else:
                    copy(inter_tail[0:TAIL, :], gate[0:TAIL, j % 2, :]).then_inc(inter_hi, 1)

            program(act, {"consts": consts, "wsum": wsum, "wsign": wsign, "split_ctx": split_ctx, "split_ctxT": split_ctxT,
                          "kcopy": kcopy, "split_q": split_q, "kexp": kexp, "kparts": kparts, "cparts": cparts,
                          "mparts": mparts, "qsub": qsub, "e": e, "y": y_, "nroot": nroot, "z": z, "zt": zt,
                          "inter": inter_})

        @block.vector
        def _(dve):
            def minus(out_ap, a, b_ap):
                return nc.vector.tensor_tensor(out_ap, a, b_ap, ALU.subtract)

            def consts():
                nc.vector.memset(absum[:, :, :], 0.0).then_inc(wsum_zero, 1)
                dve.wait_ge(attw_hi, 2)
                minus(wq_lo[:, :], kT[:, 0, :], wq_hi[:, :]).then_inc(attw_lo, 1)
                minus(wk_lo[:, :], kT[:, 1, :], wk_hi[:, :]).then_inc(attw_lo, 1)
                dve.wait_ge(a_hi_s, 1)
                minus(a_lo[:, :, :].rearrange("p h o -> p (h o)"),
                      ps[:, A0:A0 + 2, :].rearrange("p a c -> p (a c)"),
                      a_hi[:, :, :].rearrange("p h o -> p (h o)")).then_inc(a_lo_s, 1)
                dve.wait_ge(tanh_done, 1)
                nc.vector.scalar_tensor_tensor(out=small[:, COEF_X:COEF_X + 1], in0=small[:, GX:GX + 1],
                                               scalar=float(P) ** 0.5, in1=small[:, TX:TX + 1], op0=ALU.mult,
                                               op1=ALU.mult).then_inc(coef_x, 1)

            def wsum(m, c):
                if c in SUM_ACT:
                    return
                step = ("wsum", m, c)
                s, n = staged(step)
                dve.wait_ge(s_load_w[s], n)
                if m == 0:
                    dve.wait_ge(wsum_zero, 1)
                v = stage_view(step)
                nc.vector.tensor_reduce(absum[0:v.shape[0], m, c:c + 1], v, AX_X, ALU.add,
                                        apply_absolute_value=True).then_inc(wsum_dve, 1)

            def wscale(m):
                dve.wait_ge(wsum_act, (m + 1) * len(SUM_ACT))
                dve.wait_ge(wsum_dve, (m + 1) * (IC + 1 - len(SUM_ACT)))
                nc.vector.tensor_reduce(wtot[:, m:m + 1], absum[:, m, :], AX_X, ALU.add).then_inc(wpart, 1)
                dve.wait_ge(wall, m + 1)
                nc.vector.tensor_scalar(wthr[:, m, 0:1], wtot[:, m:m + 1], 1.0 / (I * N), None,
                                        ALU.mult).then_inc(wthr_done, 1)
                dve.wait_ge(wthr_done, 3 * m + 1)
                nc.vector.tensor_scalar(wthr[:, m, 1:2], wthr[:, m, 0:1], EPS, None,
                                        ALU.add).then_inc(wthr_done, 1)
                dve.wait_ge(wthr_done, 3 * m + 2)
                nc.vector.reciprocal(wthr[:, m, 2:3], wthr[:, m, 1:2]).then_inc(wthr_done, 1)
                if m == DOWN:
                    dve.wait_ge(wthr_done, 9)
                    nc.vector.scalar_tensor_tensor(out=small[:, SC:SC + 1], in0=wthr[:, GATE, 0:1],
                                                   scalar=1.0 / I_SCALE, in1=wthr[:, UP, 0:1], op0=ALU.mult,
                                                   op1=ALU.mult).then_inc(coef_f, 1)
                    dve.wait_ge(coef_f, 1)
                    nc.vector.scalar_tensor_tensor(out=small[:, COEF_F:COEF_F + 1], in0=small[:, SC:SC + 1],
                                                   scalar=small[:, TF:TF + 1], in1=wthr[:, DOWN, 0:1],
                                                   op0=ALU.mult, op1=ALU.mult).then_inc(coef_f, 1)

            def wquant(m, c):
                step = ("wquant", m, c)
                s, n = staged(step)
                dve.wait_ge(s_load_w[s], n)
                dve.wait_ge(wthr_done, 3 * m + 3)
                v = stage_view(step)
                nc.vector.tensor_scalar(v, v, wthr[:, m, 2:3], ROUND, ALU.mult, ALU.add).then_inc(w_rounded, 1)

            def split_ctx(bt, b, _):
                wait(dve, c_hi, bt.count(1, 1))
                minus(in_lo[:, :], raw[:, :], in_hi[:, :]).then_inc(c_lo, 1)

            def split_ctxT(bt, b, _):
                wait(dve, ct_hi_s, bt.count(1, 1))
                minus(ct_lo[:, :], rawT[:, :], ct_hi[:, :]).then_inc(ct_lo_s, 1)

            def row_stats(done, bt, b, m):
                for h in range(2):
                    nc.vector.bn_stats(stats[:, h, :], xb_ring[:, b, h * 512:h * 512 + 512]).then_inc(done, 1)
                wait(dve, done, bt.count(4, 2))
                settle(dve, settled)
                nc.vector.bn_aggr(m[:, 0:2], stats[:, :, :].rearrange("p a b -> p (a b)")).then_inc(done, 1)
                wait(dve, done, bt.count(4, 3))
                nc.vector.tensor_scalar(m[:, 2:3], m[:, 1:2], EPS, None, ALU.add).then_inc(done, 1)

            def ln1_(bt, b, _):
                wait(dve, x_in, bt.count(16, 16))
                wait(dve, q32, bt.count(1, 0))
                row_stats(ln1, bt, b, mv)

            def q32_(bt, b, _):
                wait(dve, rstd1, bt.count(1, 1))
                wait(dve, kt_ready, bt.count(8, 8))
                nc.vector.tensor_scalar(raw[:, :], xb_ring[:, b, :], mv[:, 0:1], mv[:, 3:4], ALU.subtract,
                                        ALU.mult).then_inc(q32, 1)

            def split_q(bt, b, _):
                wait(dve, q_hi, bt.count(1, 1))
                minus(in_lo[:, :], raw[:, :], in_hi[:, :]).then_inc(q_lo, 1)

            def kcopy(bt, b, c):
                if c == 0:
                    return
                wait(dve, kt_copied, bt.count(8, c + 1))
                if c == 1:
                    wait(dve, denom_ready, bt.count(1, 0))
                else:
                    wait(dve, kmax_step, bt.count(7, c - 1))
                nc.vector.tensor_tensor(kstat[:, :], kT[:, 0, :] if c == 1 else kstat[:, :], kT[:, c, :],
                                        ALU.max).then_inc(kmax_step, 1)

            def kparts(bt, b, c):
                wait(dve, k_hi, bt.count(8, c + 1))
                wait(dve, ctxk_done, bt.count(8, c - 1))
                minus(k_lo_b[:, c % 2, :], kT[:, c, :], k_hi_b[:, c % 2, :]).then_inc(k_lo, 1)

            def ztotal(bt, b, _):
                wait(dve, denom_ready, bt.count(1, 1))
                wait(dve, m_scaled, bt.count(2, 0))
                nc.vector.reciprocal(k_rec_b, ps[:, A2, 0:PAIRS]).then_inc(k_rec, 1)

            def cparts(bt, b, _):
                wait(dve, cc_hi, bt.count(1, 1))
                minus(cc_lo_b, ps[:, A3, :], cc_hi_b).then_inc(cc_lo, 1)

            def mparts(bt, b, _):
                wait(dve, m_ready, bt.count(1, 1))
                wait(dve, out_ready, bt.count(2, 0))
                for s in range(2):
                    r = slice(s * DH, s * DH + DH)
                    wait(dve, k_rec, bt.count(1, 1))
                    nc.vector.tensor_tensor(m32[r, :, :], mt_psum(r, s),
                                            k_rec_b[r, :].unsqueeze(2).broadcast_to([DH, PAIRS, P]),
                                            ALU.mult).then_inc(m_scaled, 1)
                for s in range(2):
                    r = slice(s * DH, s * DH + DH)
                    wait(dve, mt_hi, bt.count(2, s + 1))
                    minus(mt_lo_b[r, :, :], m32[r, :, :], mt_hi_b[r, :, :]).then_inc(mt_lo, 1)

            def per_head(ap):
                return ap.rearrange("p (h d) -> p h d", h=HEADS)

            def spread(ap):
                return ap.unsqueeze(2).broadcast_to([P, HEADS, DH])

            def qsub(bt, b, c):
                wait(dve, qt_ready, bt.count(8, c + 1))
                t = ps[:, A0 + c % 2, :]
                nc.vector.tensor_reduce(q_stat[:, c % QR, 0, :], per_head(t), AX_X, ALU.max).then_inc(q_max, 1)
                wait(dve, q_max, bt.count(8, c + 1))
                wait(dve, tr_ready, bt.count(8, c - QR + 1))
                nc.vector.tensor_tensor(per_head(qs[:, c % QR, :]), per_head(t), spread(q_stat[:, c % QR, 0, :]),
                                        ALU.subtract).then_inc(q_shifted, 1)

            def qsum(bt, b, c):
                wait(dve, q_exp, bt.count(8, c + 1))
                nc.vector.tensor_reduce(q_stat[:, c % QR, 1, :], per_head(qs[:, c % QR, :]), AX_X,
                                        ALU.add).then_inc(q_sum, 1)
                wait(dve, q_sum, bt.count(8, c + 1))
                wait(dve, q_prob, bt.count(8, c - QR + 1))
                nc.vector.reciprocal(q_stat[:, c % QR, 1, :], q_stat[:, c % QR, 1, :]).then_inc(q_rec, 1)

            def e(bt, b, c):
                wait(dve, e_hi, bt.count(8, c + 1))
                o = (c % 4) * P
                minus(e_lo_b[:, :, o:o + P], ps[:, A2, :].rearrange("p (a c) -> p a c", a=PAIRS),
                      e_hi_b[:, :, o:o + P]).then_inc(e_lo, 1)

            def nroot(bt, b, hf):
                wait(dve, rs_ready, bt.count(2, hf + 1))
                nc.vector.tensor_scalar(sq[:, :], sq[:, :], 1e-12, None, ALU.max).then_inc(rs_guarded, 1)
                wait(dve, rs_guarded, bt.count(2, hf + 1))
                nc.vector.reciprocal(sq[:, 0:256], sq[:, 0:256]).then_inc(rs_inverse, 1)

            def nrec(bt, b, hf):
                wait(dve, rs_guarded, bt.count(2, hf + 1))
                nc.vector.reciprocal(sq[:, 256:512], sq[:, 256:512]).then_inc(rs_inverse, 1)

            def norm(bt, b, hf):
                wait(dve, rs_inverse, bt.count(4, 2 * hf + 2))
                wait(dve, y_ready, bt.count(2, hf + 1))
                nc.vector.tensor_tensor(y[:, :], y[:, :], sq[:, :], ALU.mult).then_inc(y_scaled, 1)
                wait(dve, y_scaled, bt.count(2, hf + 1))
                wait(dve, coef_x, 1)
                v = xb_ring[:, b, hf * 512:hf * 512 + 512]
                wait(dve, q32, bt.count(1, 1))
                nc.vector.scalar_tensor_tensor(out=v, in0=y[:, :], scalar=small[:, COEF_X:COEF_X + 1], in1=v,
                                               op0=ALU.mult, op1=ALU.add).then_inc(x2_ready, 1)

            def ln2_(bt, b, _):
                wait(dve, x2_ready, bt.count(2, 2))
                wait(dve, z32, bt.count(1, 0))
                row_stats(ln2, bt, b, mv2)

            def z(bt, b, _):
                wait(dve, rstd2, bt.count(1, 1))
                nc.vector.tensor_scalar(mv2[:, 2:3], mv2[:, 3:4], Z_SCALE, None, ALU.mult).then_inc(z_rstd, 1)
                wait(dve, z_rstd, bt.count(1, 1))
                wait(dve, x2_stored, bt.count(16, 16))
                v = xb_ring[:, b, :]
                nc.vector.tensor_scalar(v, v, mv2[:, 0:1], mv2[:, 2:3], ALU.subtract,
                                        ALU.mult).then_inc(z32, 1)
                wait(dve, z_hi_s, bt.count(1, 1))
                minus(z_lo[:, b, :], v, z_hi[:, b, :]).then_inc(z_lo_s, 1)

            def zt(nxt, b):
                wait(dve, gu_ready, nxt.count(J, 0))
                wait(dve, zt_ready, nxt.count(4, 2 * b + 2))
                nc.vector.tensor_copy(zT[:, 1, :, b * P:b * P + P],
                                      ps[:, ZT_BANKS[b][1], :].bitcast(F16).rearrange("p (k t) -> p k t", k=NC)
                                      ).then_inc(zt_lo, 1)

            def inter_(grp, j):
                wait(dve, gate_copied, grp.count(J, j + 1))
                r = slice(0, P if j < IC else TAIL)
                other = ps[r, j % 2, T:2 * T] if j < IC else ps[r, j % 2, 0:T]
                nc.vector.scalar_tensor_tensor(out=gate[r, j % 2, :], in0=other, scalar=I_SCALE / Z_SCALE,
                                               in1=gate[r, j % 2, :], op0=ALU.mult,
                                               op1=ALU.mult).then_inc(inter32, 1)
                if j:
                    inter_low(grp, j - 1)
                if j == IC:
                    inter_low(grp, j)

            def inter_low(grp, j):
                wait(dve, inter_hi, grp.count(J, j + 1))
                if j < IC:
                    minus(inter[:, j, 1, :], gate[:, j % 2, :], inter[:, j, 0, :]).then_inc(inter_lo, 1)
                else:
                    minus(inter_tail[TAIL:2 * TAIL, :], gate[0:TAIL, j % 2, :],
                          inter_tail[0:TAIL, :]).then_inc(inter_lo, 1)

            def finish(grp, b):
                for hf in range(2):
                    wait(dve, down_ready, grp.count(4, 2 * b + hf + 1))
                    wait(dve, x2_back[hf], grp.count(32, 16 * b + 16))
                    wait(dve, coef_f, 2)
                    nc.vector.scalar_tensor_tensor(out=fin[:, hf, :], in0=ps[:, (2 if b == 0 else 0) + hf, :],
                                                   scalar=small[:, COEF_F:COEF_F + 1], in1=fin[:, hf, :],
                                                   op0=ALU.mult, op1=ALU.add).then_inc(fin_ready, 1)

            program(dve, {"consts": consts, "wsum": wsum, "wscale": wscale, "wquant": wquant,
                          "split_ctx": split_ctx, "split_ctxT": split_ctxT, "ln1": ln1_,
                          "q32": q32_, "kcopy": kcopy, "split_q": split_q, "kparts": kparts, "ztotal": ztotal,
                          "cparts": cparts, "mparts": mparts, "qsub": qsub, "qsum": qsum, "e": e, "nroot": nroot, "nrec": nrec, "norm": norm,
                          "ln2": ln2_, "z": z, "zt": zt, "inter": inter_, "finish": finish})

        @block.gpsimd
        def _(pool):
            def consts():
                nc.gpsimd.memset(neg_half[:, :], -0.5).then_inc(started, 1)
                nc.gpsimd.memset(ones[:, :], 1.0).then_inc(started, 1)
                nc.gpsimd.memset(minus_round[:, :], -ROUND).then_inc(round_set, 1)

            def rstd(bt, stat, m, done):
                wait(pool, started, 2)
                wait(pool, stat, bt.count(4, 4))
                nc.gpsimd.tensor_tensor(m[:, 3:4], m[:, 2:3], neg_half[:, :], ALU.pow).then_inc(done, 1)

            def ln1_(bt, b, _):
                rstd(bt, ln1, mv, rstd1)

            def ln2_(bt, b, _):
                rstd(bt, ln2, mv2, rstd2)

            def wscale(m):
                pool.wait_ge(wpart, m + 1)
                nc.gpsimd.partition_all_reduce(wtot[:, m:m + 1], wtot[:, m:m + 1], P, RADD).then_inc(wall, 1)

            def kmax(bt, b, _):
                wait(pool, kmax_step, bt.count(7, 7))
                settle(pool, settled)
                nc.gpsimd.partition_all_reduce(kstat[:, :], kstat[:, :], P, RMAX).then_inc(kmax_all, 1)

            def kshift(bt, b, i):
                wait(pool, kmax_all, bt.count(1, 1))
                v = kT[:, 2 * i:2 * i + 2, :]
                nc.gpsimd.tensor_tensor(v, v, kstat[:, :].unsqueeze(1).broadcast_to([P, 2, HD]),
                                        ALU.subtract).then_inc(k_shifted, 1)

            def ksum(bt, b, i):
                wait(pool, k_exp, bt.count(4, (i + 1) // 2 + 1))
                if i == 0:
                    wait(pool, k_shifted, bt.count(4, 4))
                else:
                    wait(pool, ksum_step, bt.count(7, i))
                nc.gpsimd.tensor_tensor(kstat[:, :], kT[:, 0, :] if i == 0 else kstat[:, :], kT[:, i + 1, :],
                                        ALU.add).then_inc(ksum_step, 1)

            def qsum(bt, b, c):
                wait(pool, q_rec, bt.count(8, c + 1))
                v = qs[:, c % QR, :].rearrange("p (h d) -> p h d", h=HEADS)
                nc.gpsimd.tensor_tensor(v, v, q_stat[:, c % QR, 1, :].unsqueeze(2).broadcast_to([P, HEADS, DH]),
                                        ALU.mult).then_inc(q_prob, 1)

            def y_(bt, b, hf):
                wait(pool, sq_ready, bt.count(2, hf + 1))
                settle(pool, settled)
                nc.gpsimd.partition_all_reduce(sq[:, :], sq[:, :], P, RADD).then_inc(sqsum, 1)

            program(pool, {"consts": consts, "ln1": ln1_, "ln2": ln2_, "wscale": wscale, "kmax": kmax, "kshift": kshift, "ksum": ksum, "qsum": qsum,
                           "y": y_})


def kernel(**inputs):
    import numpy as np
    import concourse.bacc as bacc
    from concourse.bass_utils import run_bass_kernel_spmd

    nc = bacc.Bacc("TRN2", target_bir_lowering=False, num_devices=1)
    f = {k: np.asarray(v) for k, v in inputs.items()}

    def chunked(w):
        t = w.T.reshape(NC, P, I).transpose(1, 0, 2)
        full = t[:, :, :IC * P].reshape(P, NC, IC, P).transpose(0, 2, 1, 3).reshape(P, IC * CH)
        return np.concatenate([full, t[:, :, IC * P:].reshape(P, NC * TAIL)], axis=1)

    down_t = f["L0_ffn_w_down"].T
    arrays = {
        "x": f["x"],
        "ctxn": f["ctx_4096"],
        "ctxt": f["ctx_4096"].transpose(0, 2, 1).reshape(B, NC, P, P).transpose(0, 2, 1, 3),
        "wq": f["L0_xattn_Wq"].T,
        "wk": f["L0_xattn_Wk"].T,
        "wv": f["L0_xattn_Wv"].reshape(HEADS, DH, P).transpose(1, 0, 2).reshape(DH, HEADS * P),
        "wo": f["L0_xattn_Wo"].T.reshape(HEADS, DH, P).transpose(1, 0, 2).reshape(DH, HEADS * P),
        "bo": f["L0_xattn_bo"].reshape(P, 1),
        "gx": f["L0_xattn_g"].reshape(P, 1),
        "g_xattn": np.broadcast_to(f["g_xattn"].reshape(1, 1), (P, 1)),
        "g_ffn": np.broadcast_to(f["g_ffn"].reshape(1, 1), (P, 1)),
        "gate_w": chunked(f["L0_ffn_w_gate"]),
        "up_w": chunked(f["L0_ffn_w_up"]),
        "down_w": down_t[:IC * P].reshape(IC, P, N).transpose(1, 0, 2).reshape(P, IC * N),
        "down_tail": down_t[IC * P:],
        "ident": np.eye(P, dtype=np.float32),
    }
    arrays = {f"in_{k}": np.ascontiguousarray(v) for k, v in arrays.items()}
    args = [nc.dram_tensor(k, v.shape, mybir.dt.from_np(v.dtype), kind="ExternalInput").ap()
            for k, v in arrays.items()]
    args.append(nc.dram_tensor("out", (B, P, N), F32, kind="ExternalOutput").ap())
    gated_attention_ffn(nc, *args)
    r = run_bass_kernel_spmd(nc, [arrays], core_ids=[0])
    return r.results[0]["out"]
```
